# Optimizing a Trainium2 kernel written in Bass

```python
import numpy as np
import jax
import jax.numpy as jnp

def _softmax(x, axis=-1):
    return jax.nn.softmax(x, axis=axis)

def _gelu(x):
    return jax.nn.gelu(x, approximate=True)

def _silu(x):
    return jax.nn.silu(x)

def _sigmoid(x):
    return jax.nn.sigmoid(x)

def _layernorm(x, axis=-1, eps=1e-05):
    m = jnp.mean(x, axis=axis, keepdims=True)
    v = jnp.var(x, axis=axis, keepdims=True)
    return (x - m) / jnp.sqrt(v + eps)

def _scatter_add(tgt, idx, src, axis=0):
    return tgt.at[idx].add(src)

def _segment_sum(src, seg, n):
    return jax.ops.segment_sum(src, seg, n)
kernel_name = 'mk_flamingo_gated_d1_seqx_r2_332460'

def setup_inputs(seed: int=0):
    np.random.seed(seed)
    _w = jnp.asarray

    def _rec_inputs():
        import jax
        import jax.numpy as jnp
        _rk = jax.random.key(seed)
        x = -0.000125 + 0.9999 * jax.random.normal(jax.random.fold_in(_rk, 1), (8, 1024, 512), jnp.float32)
        _lenS = 1024 - jax.random.randint(jax.random.fold_in(_rk, 7), (8,), 0, max(1, 1024 // 4) + 1, jnp.int32)
        _lenS2 = 1024 - jax.random.randint(jax.random.fold_in(_rk, 8), (8,), 0, max(1, 1024 // 4) + 1, jnp.int32)
        _ctx_1024P = jax.random.normal(jax.random.fold_in(_rk, 11), (8, 16, 512), jnp.float32)
        _ctx_1024c = jax.random.dirichlet(jax.random.fold_in(_rk, 511), 0.3 * jnp.ones((16,), jnp.float32), (8, 1024))
        _ctx_1024t = jnp.einsum('bsk,bkd->bsd', _ctx_1024c, _ctx_1024P)
        _ctx_1024t = _ctx_1024t * jax.lax.rsqrt(jnp.mean(jnp.square(_ctx_1024t)) + 1e-12) * 0.953939
        ctx_1024 = -1.52775e-05 + 0.999936 * (_ctx_1024t + 0.3 * jax.random.normal(jax.random.fold_in(_rk, 611), (8, 1024, 512), jnp.float32))
        _g = jax.random.normal(jax.random.fold_in(_rk, 9001), (2, 1), jnp.float32)
        _g = jnp.sign(_g) * jnp.maximum(jnp.abs(_g), 1.0) + (_g == 0) * 1.0
        g_xattn = _g[0]
        g_ffn = _g[1]
        return (x, ctx_1024, g_xattn, g_ffn)
    x, ctx_1024, g_xattn, g_ffn = _rec_inputs()

    def _L0_xattn_setup():
        import jax, jax.numpy as jnp
        import numpy as np
        D_MODEL = 512
        HEAD_SIZE = 512
        CONTEXT_SIZE = 128
        key = jax.random.key(seed)
        kq, kk, kv, kwq, kwk, kwv = jax.random.split(key, 6)
        B, S = (128, 128)
        scale = 1.0 / np.sqrt(D_MODEL)
        return {'query': jax.random.normal(kq, (B, S, D_MODEL), dtype=jnp.float32), 'key': jax.random.normal(kk, (B, S, D_MODEL), dtype=jnp.float32), 'value': jax.random.normal(kv, (B, S, D_MODEL), dtype=jnp.float32), 'w_q': jax.random.normal(kwq, (D_MODEL, HEAD_SIZE), dtype=jnp.float32) * scale, 'w_k': jax.random.normal(kwk, (D_MODEL, HEAD_SIZE), dtype=jnp.float32) * scale, 'w_v': jax.random.normal(kwv, (D_MODEL, HEAD_SIZE), dtype=jnp.float32) * scale, 'mask': 1}
    _L0_xattn_all = _L0_xattn_setup()
    _L0_xattn_in = {k: v for k, v in _L0_xattn_all.items() if k in ('w_q', 'w_k', 'w_v')}
    del _L0_xattn_all

    def _L0_ffn_setup():
        import jax, jax.numpy as jnp
        import numpy as np
        EMB = 512
        FF = 4 * EMB

        def _ternary(w):
            scale = jnp.maximum(jnp.mean(jnp.abs(w)), 1e-08)
            w_t = jnp.clip(jnp.round(w / scale), -1.0, 1.0)
            return w + jax.lax.stop_gradient(w_t - w)
        key = jax.random.key(seed)
        kx, k1, k2, kb1, kb2 = jax.random.split(key, 5)
        x = jax.random.normal(kx, (4, 1024, EMB), dtype=jnp.float32)
        lim1 = 1.0 / np.sqrt(EMB)
        lim2 = 1.0 / np.sqrt(FF)
        W1 = jax.random.uniform(k1, (FF, EMB), jnp.float32, -lim1, lim1)
        b1 = jax.random.uniform(kb1, (FF,), jnp.float32, -lim1, lim1)
        W2 = jax.random.uniform(k2, (EMB, FF), jnp.float32, -lim2, lim2)
        b2 = jax.random.uniform(kb2, (EMB,), jnp.float32, -lim2, lim2)
        return {'x': x, 'W1': W1, 'b1': b1, 'W2': W2, 'b2': b2}
    _L0_ffn_all = _L0_ffn_setup()
    _L0_ffn_in = {k: v for k, v in _L0_ffn_all.items() if k in ('W1', 'b1', 'W2', 'b2')}
    del _L0_ffn_all
    return {'x': x, 'ctx_1024': ctx_1024, 'g_xattn': g_xattn, 'g_ffn': g_ffn, 'L0_xattn_w_q': _L0_xattn_in['w_q'], 'L0_xattn_w_k': _L0_xattn_in['w_k'], 'L0_xattn_w_v': _L0_xattn_in['w_v'], 'L0_ffn_W1': _L0_ffn_in['W1'], 'L0_ffn_b1': _L0_ffn_in['b1'], 'L0_ffn_W2': _L0_ffn_in['W2'], 'L0_ffn_b2': _L0_ffn_in['b2']}

def reference(x, ctx_1024, g_xattn, g_ffn, L0_xattn_w_q, L0_xattn_w_k, L0_xattn_w_v, L0_ffn_W1, L0_ffn_b1, L0_ffn_W2, L0_ffn_b2):
    import jax
    import jax.numpy as jnp

    def _L0_xattn_ref(query, key, value, w_q, w_k, w_v, mask):
        import jax, jax.numpy as jnp
        import numpy as np
        D_MODEL = 512
        HEAD_SIZE = 512
        CONTEXT_SIZE = 128
        q = jnp.einsum('bsd,dh->bsh', query, w_q)
        k = jnp.einsum('bsd,dh->bsh', key, w_k)
        v = jnp.einsum('bsd,dh->bsh', value, w_v)
        scale = 1.0 / np.sqrt(query.shape[-1]).astype(np.float32)
        scores = jnp.einsum('bqh,bkh->bqk', q, k) * scale
        if mask:
            S = scores.shape[1]
            causal = jnp.tril(jnp.ones((S, S), dtype=bool))
            scores = jnp.where(causal, scores, -jnp.inf)
        attn = jax.nn.softmax(scores, axis=-1)
        out = jnp.einsum('bqk,bkh->bqh', attn, v)
        return out

    def _L0_ffn_ref(x, W1, b1, W2, b2):
        import jax, jax.numpy as jnp
        import numpy as np
        EMB = 512
        FF = 4 * EMB

        def _ternary(w):
            scale = jnp.maximum(jnp.mean(jnp.abs(w)), 1e-08)
            w_t = jnp.clip(jnp.round(w / scale), -1.0, 1.0)
            return w + jax.lax.stop_gradient(w_t - w)
        h = jnp.einsum('bsd,fd->bsf', x, _ternary(W1)) + b1
        h = jax.nn.gelu(h, approximate=False)
        out = jnp.einsum('bsf,df->bsd', h, _ternary(W2)) + b2
        return out
    x = x + jnp.tanh(g_xattn[0]) * _L0_xattn_ref(_layernorm(x, axis=-1), ctx_1024, ctx_1024, L0_xattn_w_q, L0_xattn_w_k, L0_xattn_w_v, 1)
    x = x + jnp.tanh(g_ffn[0]) * _L0_ffn_ref(_layernorm(x, axis=-1), L0_ffn_W1, L0_ffn_b1, L0_ffn_W2, L0_ffn_b2)
    return x

_drawn_inputs = setup_inputs


def setup_inputs(seed=0):
    import zlib

    import numpy as np

    out = dict(_drawn_inputs(seed))
    spreads = {}
    factors = {'L0_ffn_b1': 46.254, 'L0_ffn_b2': 64.0}
    for name, (base, spread) in spreads.items():
        noise = np.random.default_rng([zlib.crc32(name.encode()), seed]).standard_normal(out[name].shape)
        drawn = base * np.exp(spread * noise) if base else spread * noise
        out[name] = jnp.asarray(drawn.astype(out[name].dtype))
    for name, factor in factors.items():
        out[name] = (out[name] * factor).astype(out[name].dtype)
    return out
```

```python
from contextlib import ExitStack
import math

import concourse.bass as bass
from concourse import mybir

ALU = mybir.AluOpType
ACT = mybir.ActivationFunctionType
AX = mybir.AxisListType
F32 = mybir.dt.float32
F16 = mybir.dt.float16
I32 = mybir.dt.int32
RMAX = bass.bass_isa.ReduceOp.max
RADD = bass.bass_isa.ReduceOp.add

P = 128
HI, LO = 0, 1
PASSES = ((HI, HI), (LO, HI), (HI, LO))


def gated_block(nc, x, ctxT, g_xattn, g_ffn, wqT, wkT, wv, w1T, b1c, w2T, b2, out):
    B, _, DC, S = ctxT.shape
    N, D = x.shape
    FC = b1c.shape[1]
    NT = N // P
    TB = S // P
    BODY = 2 * TB
    TURNS = NT // BODY
    GT = 4
    NG = NT // GT
    EPS = 1e-5
    NEG = -3.0e38

    XN = 2.0 ** 10
    TOP = 2.0 ** 13
    T_DOWN = 2.0 ** -18
    V_DOWN = 2.0 ** -22
    P_UP = 2.0 ** 14
    G_TOP = 2.0 ** 14
    TINY = 2.0 ** -40

    x_tiles = x.rearrange("(t p) d -> t p d", p=P)
    out_tiles = out.rearrange("(t p) d -> t p d", p=P)

    es = ExitStack()
    with es:
        def sb(name, shape, dt=F32):
            return es.enter_context(nc.sbuf_tensor(name, shape, dt))

        def ps(name, shape, dt=F32):
            return es.enter_context(nc.psum_tensor(name, shape, dt))

        def sem(name):
            return es.enter_context(nc.semaphore(name))

        a_s = sb("a_s", [P, 2, DC, D], F16)
        wv_s = sb("wv_s", [P, 2, DC, D], F16)
        raw = sb("raw", [P, DC * S])
        ctx_s = sb("ctx_s", [P, 2, 2, DC, S], F16)
        tT = sb("tT", [P, 2, 2, DC, 2 * P], F16)
        v_s = sb("v_s", [P, 2, 2, TB, D], F16)
        xnT = sb("xnT", [P, 2, 2, DC, 2 * P], F16)
        x_ring = sb("x_ring", [P, 8, D])
        xn32 = sb("xn32", [P, 2, D])
        xn_s = sb("xn_s", [P, 2, 2, D], F16)
        p32 = sb("p32", [P, S])
        p_s = sb("p_s", [P, 2, S], F16)
        pT = sb("pT", [P, 2, S], F16)
        x2_ring = sb("x2_ring", [P, 4, D])
        w1_s = sb("w1_s", [P, DC, FC * P], F16)
        w2_s = sb("w2_s", [P, FC, D], F16)
        WCH = 1024
        w_in = sb("w_in", [P, 2, WCH])
        w_neg = sb("w_neg", [P, WCH], F16)
        g32 = sb("g32", [P, 2, 4 * P])
        b2_row = sb("b2_row", [P, D])
        b1_s = sb("b1_s", [P, FC])
        ident = sb("ident", [P, P], F16)
        causal = sb("causal", [P, P])
        bn6 = sb("bn6", [P, 2, 6])
        mv = sb("mv", [P, 2, 2])
        var_s = sb("var_s", [P, 2])
        rstd = sb("rstd", [P, 2])
        minus_half = sb("minus_half", [P, 1])
        negmax = sb("negmax", [P, 2])
        ebias = sb("ebias", [P, 2])
        rowsum = sb("rowsum", [P, 2])
        rinv = sb("rinv", [P, 2])
        osc = sb("osc", [P, 2])
        cmax = sb("cmax", [P, 2])
        call = sb("call", [P, 2])
        sc = sb("sc", [P, 32])
        esc = sb("esc", [P, 2])
        fsc = sb("fsc", [P, 2])
        csc = sb("csc", [P, 1])
        wsum = sb("wsum", [P, 16])
        wtot = sb("wtot", [P, 4])

        wqk_in = ctx_s[:, 1, :, :, :].rearrange("p a c s -> p (a c s)").bitcast(F32) \
            .rearrange("p (w c d) -> p w c d", w=2, c=DC)
        prod_in = v_s[:, 1, :, :, :].rearrange("p a t d -> p (a t d)").bitcast(F32) \
            .rearrange("p (w c d) -> p w c d", w=2, c=DC)
        a32, wv32 = prod_in[:, 0], prod_in[:, 1]

        x2_in = raw[:, :].rearrange("p (t d) -> p t d", d=D)
        yT = ctx_s[:, 0, :, :, :].rearrange("p a c s -> p (a c s)") \
            .rearrange("p (g a c n) -> p g a c n", g=2, a=2, c=DC)
        v_old = v_s[:, 0, :, :, :].rearrange("p a t d -> p (a t d)")
        g_s = v_old[:, 0:4 * 2 * 512].rearrange("p (r a n) -> p r a n", r=4, a=2)
        y_out = v_old[:, 4096:8192].bitcast(F32).rearrange("p (t d) -> p t d", d=D)

        s_ps = ps("s_ps", [P, S])
        pT_ps = ps("pT_ps", [P, 2, S], F16)
        v_ps = ps("v_ps", [P, D])
        t_ps = ps("t_ps", [P, 2, 2 * P])
        o_ps = ps("o_ps", [P, D])
        xT_ps = ps("xT_ps", [P, 2, DC, P], F16)
        a_ps = [s_ps[:, 0:D], s_ps[:, D:2 * D], v_ps[:, :], o_ps[:, :]]
        pT32 = pT_ps[:, :, :].rearrange("p a n -> p (a n)").bitcast(F32)
        y_ps = [s_ps[:, 0:D], s_ps[:, D:2 * D], pT32[:, 0:D], pT32[:, D:2 * D]]
        h_ps = [v_ps[:, :], o_ps[:, :]]

        x_in = [sem(f"x_in{i}") for i in range(8)]
        ctx_in = sem("ctx_in")
        w_qk_in, w_v_in, small_in = sem("w_qk_in"), sem("w_v_in"), sem("small_in")
        consts = sem("consts")
        a_mm, a_evac = sem("a_mm"), sem("a_evac")
        wmax, wmax_all = sem("wmax"), sem("wmax_all")
        link = sem("link")
        w_scaled, a_hi, weights_split = sem("w_scaled"), sem("a_hi"), sem("weights_split")
        tanh_done = sem("tanh_done")
        ctx_max, ctx_max_all, ctx_scaled = sem("ctx_max"), sem("ctx_max_all"), sem("ctx_scaled")
        ctx_hi, ctx_split = sem("ctx_hi"), sem("ctx_split")
        bn_done, aggr_done, ln_var, ln_rstd = sem("bn_done"), sem("aggr_done"), sem("ln_var"), sem("ln_rstd")
        xn_ready, xn_hi, xn_lo = sem("xn_ready"), sem("xn_hi"), sem("xn_lo")
        x_tr, xT_ready = sem("x_tr"), sem("xT_ready")
        t_mm, t_hi, t_split = sem("t_mm"), sem("t_hi"), sem("t_split")
        v_mm, v_hi, v_split = sem("v_mm"), sem("v_hi"), sem("v_split")
        s_mm, s_masked, s_max, s_bias = sem("s_mm"), sem("s_masked"), sem("s_max"), sem("s_bias")
        p_exp, p_hi, p_split = sem("p_exp"), sem("p_hi"), sem("p_split")
        p_tr, pT_ready = sem("p_tr"), sem("pT_ready")
        pv_mm, o_inv, o_scaled, o_done = sem("pv_mm"), sem("o_inv"), sem("o_scaled"), sem("o_done")
        x2_stored = [sem(f"x2_stored{i}") for i in range(4)]
        w_loaded = [sem(f"w_loaded{i}") for i in range(2)]
        w_summed, w_total, w_total_all, w_thresh = sem("w_summed"), sem("w_total"), sem("w_total_all"), sem("w_thresh")
        w_negs, w_ternary = sem("w_negs"), sem("w_ternary")
        x2_loaded = [sem(f"x2_loaded{i}") for i in range(8)]
        x2_biased = sem("x2_biased")
        h_mm, g_act, g_hi, g_split = sem("h_mm"), sem("g_act"), sem("g_hi"), sem("g_split")
        y_mm, y_done = sem("y_mm"), sem("y_done")
        y_stored = [sem(f"y_stored{i}") for i in range(4)]

        (C_TANH0, C_TANH1, C_G0, C_G1, C_AMAX, C_WMAX, C_BMAX, C_PA, C_PW, C_PG, C_SA, C_SW, C_SG,
         C_EA, C_FW, C_FG, C_TH1, C_NTH1, C_TH2, C_NTH2, C_CM, C_CP, C_CR, C_ALL) = range(24)

        def col(c, n=1):
            return sc[:, c:c + n]

        ctx_batches = ctxT
        LN_LEAD, XT_LEAD, T_LEAD = 5, 4, 2
        FIRST_SLOT = -LN_LEAD
        SUM_SLOT, TERN_SLOT = NT - 15, NT - 7

        CTX_SPLITS = {5: (0,), 6: (1, 2), 7: (3,)}

        def ctx_step(s):
            return s % TB

        W_CHUNKS = [(src, dst, k) for src, dst in ((w1T, w1_s), (w2T, w2_s)) for k in range(DC * FC * P // WCH)]
        NW = len(W_CHUNKS)

        def w_dst(n):
            _, dst, k = W_CHUNKS[n % NW]
            return dst[:, :, :].rearrange("p a n -> p (a n)")[:, k * WCH:(k + 1) * WCH]

        LN_STEPS = (2, 5, 8, 11)
        XT_STEPS = (4, 7, 10, 13)

        block = es.enter_context(nc.Block())

        @block.sync
        def _(sp):
            sp.dma_start(raw[:, :], ctx_batches[0].rearrange("p c s -> p (c s)")).then_inc(ctx_in, 16)
            sp.dma_start(wqk_in[:, 0], wqT).then_inc(w_qk_in, 16)
            sp.dma_start(wqk_in[:, 1], wkT).then_inc(w_qk_in, 16)
            sp.dma_start(wv32, wv).then_inc(w_v_in, 16)
            for t in range(8):
                sp.dma_start(x_ring[:, t], x_tiles[t]).then_inc(x_in[t], 16)

            def load_ctx(batch):
                sp.wait_ge(ctx_split, 4 * batch)
                sp.dma_start(raw[:, :], ctx_batches[batch].rearrange("p c s -> p (c s)")).then_inc(ctx_in, 16)

            def load_weights(n):
                if n >= 2:
                    if n - 2 < NW:
                        sp.wait_ge(w_summed, n - 1)
                    else:
                        sp.wait_ge(w_ternary, n - 1 - NW)
                src, _, k = W_CHUNKS[n % NW]
                sp.dma_start(w_in[:, n % 2], src[:, k * WCH:(k + 1) * WCH]).then_inc(w_loaded[n % 2], 16)

            def load_x2(tile, u):
                sp.dma_start(x2_in[:, u], out_tiles[tile]).then_inc(x2_loaded[u], 16)

            def slot(it, s, last=False):
                t = it * BODY + s
                if not last or t + 7 < NT:
                    sp.wait_ge(o_done, t)
                    sp.dma_start(x_ring[:, (s + 7) % 8], x_tiles[t + 7]).then_inc(x_in[(s + 7) % 8], 16)
                sp.wait_ge(o_done, t)
                sp.dma_start(out_tiles[t - 1], x2_ring[:, (s - 1) % 4]).then_inc(x2_stored[(s - 1) % 4], 16)
                if s % TB == 7 and (not last or t + 9 < NT):
                    load_ctx(it * 2 + s // TB + 2)
                if last:
                    for n in range(2 * (t - SUM_SLOT), 2 * (t - SUM_SLOT) + 2):
                        load_weights(n)

            for i in range(4):
                sp.sem_inc(x2_stored[i], 16)
                sp.sem_inc(y_stored[i], 16)
            sp.sem_inc(y_done, GT)
            load_ctx(1)
            with sp.Fori(0, TURNS - 1) as it:
                for s in range(1, BODY + 1):
                    slot(it, s)
            for s in range(1, BODY + 1):
                slot(TURNS - 1, s, last=True)
                if s == BODY - 6:
                    sp.wait_ge(ctx_split, 4 * B)
                    for i in range(4):
                        sp.wait_ge(x2_stored[i], 2 * 16)
                        load_x2(i, i)
            for i in range(4):
                sp.wait_ge(x2_stored[i], 16 * (NT // 4 + 1))

            def group(it, gg, last=False):
                g = it * 2 + gg
                if not last or g + 1 < NG:
                    sp.wait_ge(y_done, (g + 1) * GT)
                    for i in range(GT):
                        load_x2(g * GT + GT + i, ((gg + 1) % 2) * GT + i)
                for i in range(GT):
                    sp.wait_ge(y_done, (g + 1) * GT + i + 1)
                    sp.dma_start(out_tiles[g * GT + i], y_out[:, i]).then_inc(y_stored[i], 16)

            with sp.Fori(0, NG // 2 - 1) as it:
                group(it, 0)
                group(it, 1)
            group(NG // 2 - 1, 0, last=True)
            group(NG // 2 - 1, 1, last=True)
            for i in range(4):
                sp.wait_ge(y_stored[i], 16 * (NG + 1))

        @block.gpsimd
        def _(pool):
            g = nc.gpsimd
            g.memset(ident[:, :], 0.0).then_inc(consts, 1)
            g.memset(causal[:, :], 0.0).then_inc(consts, 1)
            g.memset(minus_half[:, :], -0.5).then_inc(consts, 1)
            pool.wait_ge(consts, 3)
            g.affine_select(out=ident[:, :], in_=ident[:, :], compare_op=ALU.not_equal, fill=1.0, base=0,
                            pattern=[[-1, P]], channel_multiplier=1).then_inc(consts, 1)
            g.affine_select(out=causal[:, :], in_=causal[:, :], compare_op=ALU.is_ge, fill=NEG, base=0,
                            pattern=[[-1, P]], channel_multiplier=1).then_inc(consts, 1)
            pool.wait_ge(small_in, 64)
            pool.wait_ge(ctx_max, 1)
            g.partition_all_reduce(call[:, :], cmax[:, :], P, RMAX).then_inc(ctx_max_all, 1)
            pool.wait_ge(wmax, 3)
            g.partition_all_reduce(sc[:, C_ALL:C_ALL + 3], sc[:, C_AMAX:C_AMAX + 3], P, RMAX).then_inc(wmax_all, 1)

            def norm(it, s, ctx_batch=None):
                k = it * BODY + s + LN_LEAD
                r = (s + LN_LEAD) % 2
                pool.wait_ge(ln_var, k + 1)
                g.tensor_tensor(rstd[:, r:r + 1], var_s[:, r:r + 1], minus_half[:, :], ALU.pow).then_inc(ln_rstd, 1)
                pool.wait_ge(xn_hi, k + 1)
                if ctx_batch is not None:
                    pool.wait_ge(ctx_max, ctx_batch + 1)
                if s + LN_LEAD >= 2:
                    pool.wait_ge(x_tr, k - 1)
                g.tensor_tensor(xn_s[:, r, LO], xn32[:, r], xn_s[:, r, HI], ALU.subtract).then_inc(xn_lo, 1)

            def slot(it, s, last=False):
                t = it * BODY + s
                reduce_ctx = s > 0 and ctx_step(s) == 3 and (not last or t + TB < NT)
                if not last or t + LN_LEAD < NT + GT:
                    norm(it, s, it * 2 + s // TB + 1 if reduce_ctx else None)
                if last and t + LN_LEAD >= NT and t + LN_LEAD < NT + GT:
                    add_bias(t + LN_LEAD - NT, t + LN_LEAD - NT)
                if reduce_ctx:
                    g.partition_all_reduce(call[:, :], cmax[:, :], P, RMAX).then_inc(ctx_max_all, 1)
                if last and t == TERN_SLOT - 1:
                    pool.wait_ge(w_total, 1)
                    g.partition_all_reduce(wtot[:, 2:4], wtot[:, 0:2], P, RADD).then_inc(w_total_all, 1)

            def add_bias(tile, u):
                pool.wait_ge(xn_ready, NT + tile + 1)
                g.tensor_tensor(x2_in[:, u], x2_in[:, u], b2_row[:, :], ALU.add).then_inc(x2_biased, 1)

            for s in range(FIRST_SLOT, 1):
                slot(0, s)
            with pool.Fori(0, TURNS - 1) as it:
                for s in range(1, BODY + 1):
                    slot(it, s)
            for s in range(1, BODY + 1):
                slot(TURNS - 1, s, last=True)

            def group(it, gg):
                for i in range(GT):
                    tile = it * 2 * GT + gg * GT + GT + i
                    r = i % 2
                    pool.wait_ge(ln_var, NT + tile + 1)
                    g.tensor_tensor(rstd[:, r:r + 1], var_s[:, r:r + 1], minus_half[:, :], ALU.pow).then_inc(ln_rstd, 1)
                    pool.wait_ge(xn_hi, NT + tile + 1)
                    pool.wait_ge(x_tr, NT + tile - 1)
                    g.tensor_tensor(xn_s[:, r, LO], xn32[:, r], xn_s[:, r, HI], ALU.subtract).then_inc(xn_lo, 1)
                    add_bias(tile, ((gg + 1) % 2) * GT + i)

            with pool.Fori(0, NG // 2 - 1) as it:
                group(it, 0)
                group(it, 1)
            group(NG // 2 - 1, 0)

        @block.scalar
        def _(act):
            a = nc.scalar
            act.dma_start(col(C_G0), g_xattn.partition_broadcast(P)).then_inc(small_in, 16)
            act.dma_start(col(C_G1), g_ffn.partition_broadcast(P)).then_inc(small_in, 16)
            act.dma_start(b1_s[:, :], b1c).then_inc(small_in, 16)
            act.dma_start(b2_row[:, :], b2.partition_broadcast(P)).then_inc(small_in, 16)
            act.wait_ge(small_in, 64)
            a.activation(col(C_TANH0, 2), col(C_G0, 2), ACT.Tanh).then_inc(tanh_done, 1)
            raw4 = raw[:, :].rearrange("p (c s) -> p c s", c=DC)

            def ctx_upper(batch, par, q):
                act.wait_ge(ctx_scaled, batch + 1)
                cols = slice(q * 2 * P, (q + 1) * 2 * P)
                a.activation(ctx_s[:, par, HI, :, cols], raw4[:, :, cols], ACT.Copy,
                             scale=csc[:, :]).then_inc(ctx_hi, 1)

            for q in range(4):
                ctx_upper(0, 0, q)
            for m in range(DC):
                act.wait_ge(a_mm, m + 1)
                a.activation(a32[:, m], a_ps[m], ACT.Copy).then_inc(a_evac, 1)
            act.wait_ge(w_scaled, 1)
            a.activation(wv_s[:, HI], wv32, ACT.Copy, scale=col(C_SW)).then_inc(a_hi, 1)
            a.activation(a_s[:, HI], a32, ACT.Copy, scale=col(C_SA)).then_inc(a_hi, 1)

            def softmax(it, s):
                t = it * BODY + s
                w = (s % TB + 1) * P
                r = s % 2
                act.wait_ge(s_bias, t + 1)
                act.wait_ge(p_split, t)
                a.activation(p32[:, 0:w], s_ps[:, 0:w], ACT.Exp, bias=ebias[:, r:r + 1],
                             scale=esc[:, (s // TB) % 2:(s // TB) % 2 + 1],
                             accum_out=rowsum[:, r:r + 1]).then_inc(p_exp, 1)
                act.wait_ge(p_exp, t + 1)
                act.wait_ge(p_tr, t)
                a.activation(p_s[:, HI, 0:w], p32[:, 0:w], ACT.Copy, scale=P_UP).then_inc(p_hi, 1)

            def slot(it, s, last=False):
                t = it * BODY + s
                if s >= 0 and (not last or t < NT):
                    softmax(it, s)
                if s >= -T_LEAD and (not last or t < NT - T_LEAD):
                    pr, h = ((s + T_LEAD) // 2) % 2, s % 2
                    act.wait_ge(t_mm, t + T_LEAD + 1)
                    a.activation(tT[:, pr, HI, 2 * h:2 * h + 2], t_ps[:, :, :], ACT.Copy,
                                 scale=T_DOWN).then_inc(t_hi, 1)
                if not last or t + LN_LEAD < NT + GT:
                    k = t + LN_LEAD
                    r = (s + LN_LEAD) % 2
                    act.wait_ge(xn_ready, k + 1)
                    if s + LN_LEAD >= 2:
                        act.wait_ge(x_tr, k - 1)
                    a.activation(xn_s[:, r, HI], xn32[:, r], ACT.Copy).then_inc(xn_hi, 1)
                if s > 0 and (not last or t + TB < NT):
                    for q in CTX_SPLITS.get(ctx_step(s), ()):
                        ctx_upper(it * 2 + s // TB + 1, (s // TB + 1) % 2, q)
                if s >= -1 and (not last or t + 1 < NT):
                    j, par = (s + 1) % TB, ((s + 1) // TB) % 2
                    act.wait_ge(v_mm, t + 2)
                    a.activation(v_s[:, par, HI, j], v_ps[:, :], ACT.Copy, scale=V_DOWN).then_inc(v_hi, 1)
                if s >= -XT_LEAD and (not last or t + XT_LEAD < NT + GT):
                    k = t + XT_LEAD
                    act.wait_ge(x_tr, k + 1)
                    if not last or k < NT:
                        pr, q = ((s + XT_LEAD) // 2) % 2, (s + XT_LEAD) % 2
                        dst = xnT[:, pr, :, :, q * P:(q + 1) * P]
                    else:
                        dst = yT[:, 0, :, :, (k - NT) * P:(k - NT + 1) * P]
                    a.activation(dst, xT_ps[:, :, :, :], ACT.Copy).then_inc(xT_ready, 1)
                if last and SUM_SLOT <= t < SUM_SLOT + NW // 2:
                    for n in range(2 * (t - SUM_SLOT), 2 * (t - SUM_SLOT) + 2):
                        act.wait_ge(w_loaded[n % 2], 16 * (n // 2 + 1))
                        a.activation(w_dst(n), w_in[:, n % 2], ACT.Abs,
                                     accum_out=wsum[:, n:n + 1]).then_inc(w_summed, 1)

            for s in range(FIRST_SLOT, 1):
                slot(0, s)
            with act.Fori(0, TURNS - 1) as it:
                for s in range(1, BODY + 1):
                    slot(it, s)
            for s in range(1, BODY + 1):
                slot(TURNS - 1, s, last=True)

            def hidden(F, f):
                act.wait_ge(h_mm, F + 1)
                if f >= 2:
                    act.wait_ge(g_split, F - 1)
                a.activation(g32[:, f % 2], h_ps[f % 2], ACT.Gelu, bias=b1_s[:, f % FC:f % FC + 1],
                             scale=1.0 / XN).then_inc(g_act, 1)
                act.wait_ge(g_act, F + 1)
                a.activation(g_s[:, f % 4, HI], g32[:, f % 2], ACT.Copy, scale=col(C_SG)).then_inc(g_hi, 1)

            def group(it, gg, last=False):
                for f in range(FC):
                    F = it * 2 * FC + gg * FC + f
                    if not last or F + 2 < NG * FC:
                        hidden(F + 2, f + 2)
                    if f in LN_STEPS and (not last or F + FC < NG * FC):
                        i = LN_STEPS.index(f)
                        k = NT + GT + (it * 2 + gg) * GT + i
                        act.wait_ge(xn_ready, k + 1)
                        act.wait_ge(x_tr, k - 1)
                        a.activation(xn_s[:, i % 2, HI], xn32[:, i % 2], ACT.Copy).then_inc(xn_hi, 1)
                    if f in XT_STEPS and (not last or F + FC < NG * FC):
                        i = XT_STEPS.index(f)
                        k = NT + GT + (it * 2 + gg) * GT + i
                        act.wait_ge(x_tr, k + 1)
                        a.activation(yT[:, (gg + 1) % 2, :, :, i * P:(i + 1) * P], xT_ps[:, :, :, :],
                                     ACT.Copy).then_inc(xT_ready, 1)

            hidden(0, 0)
            hidden(1, 1)
            with act.Fori(0, NG // 2 - 1) as it:
                group(it, 0)
                group(it, 1)
            group(NG // 2 - 1, 0, last=True)
            group(NG // 2 - 1, 1, last=True)

        @block.vector
        def _(dve):
            v = nc.vector
            links = [0]

            def linked(ins):
                links[0] += 1
                ins.then_inc(link, 1)
                dve.wait_ge(link, links[0])

            def power_scale(mx, pw, scale, top):
                linked(v.tensor_scalar(mx, mx, TINY, None, ALU.max))
                linked(v.tensor_scalar(pw.bitcast(I32), mx.bitcast(I32), 0x7F800000, None, ALU.bitwise_and))
                linked(v.reciprocal(scale, pw))
                linked(v.tensor_scalar(scale, scale, top, None, ALU.mult))

            raw4 = raw[:, :].rearrange("p (c s) -> p c s", c=DC)

            dve.wait_ge(ctx_in, 16)
            v.tensor_reduce(cmax[:, :], raw[:, :].rearrange("p (h n) -> p h n", h=2), AX.X, ALU.max,
                            apply_absolute_value=True).then_inc(ctx_max, 1)
            dve.wait_ge(w_v_in, 16)
            v.tensor_reduce(col(C_WMAX), wv32, AX.XY, ALU.max, apply_absolute_value=True).then_inc(wmax, 1)
            dve.wait_ge(small_in, 64)
            v.tensor_reduce(col(C_BMAX), b1_s[:, :], AX.X, ALU.max, apply_absolute_value=True).then_inc(wmax, 1)
            dve.wait_ge(ctx_max_all, 1)
            linked(v.tensor_tensor(col(C_CM), call[:, 0:1], call[:, 1:2], ALU.max))
            power_scale(col(C_CM), col(C_CP), col(C_CR), TOP)
            v.tensor_copy(csc[:, :], col(C_CR)).then_inc(ctx_scaled, 1)
            dve.wait_ge(ctx_scaled, 1)

            def ctx_lower(batch, par, q):
                dve.wait_ge(ctx_hi, 4 * batch + q + 1)
                cols = slice(q * 2 * P, (q + 1) * 2 * P)
                v.scalar_tensor_tensor(out=ctx_s[:, par, LO, :, cols], in0=raw4[:, :, cols], scalar=csc[:, :],
                                       in1=ctx_s[:, par, HI, :, cols], op0=ALU.mult,
                                       op1=ALU.subtract).then_inc(ctx_split, 1)

            for q in range(4):
                ctx_lower(0, 0, q)
            dve.wait_ge(a_evac, DC)
            v.tensor_reduce(col(C_AMAX), a32, AX.XY, ALU.max, apply_absolute_value=True).then_inc(wmax, 1)
            dve.wait_ge(wmax_all, 1)
            linked(v.tensor_scalar(col(C_ALL + 2), col(C_ALL + 2), float(D), None, ALU.add))
            power_scale(col(C_ALL, 3), col(C_PA, 3), col(C_SA, 3), TOP)
            linked(v.tensor_scalar(col(C_SG), col(C_SG), G_TOP / TOP, None, ALU.mult))
            dve.wait_ge(tanh_done, 1)
            linked(v.tensor_scalar(col(C_EA), col(C_PA), 1.0 / (XN * T_DOWN * TOP * TOP * math.sqrt(D)), None, ALU.mult))
            linked(v.tensor_scalar(col(C_FW), col(C_PW), col(C_TANH0), 1.0 / (P_UP * V_DOWN * TOP * TOP), ALU.mult, ALU.mult))
            linked(v.tensor_scalar(col(C_FG), col(C_PG), col(C_TANH1), 1.0 / G_TOP, ALU.mult, ALU.mult))
            linked(v.tensor_scalar(b2_row[:, :], b2_row[:, :], col(C_TANH1), None, ALU.mult))
            linked(v.tensor_scalar(esc[:, 0:1], col(C_EA), col(C_CP), None, ALU.mult))
            v.tensor_scalar(fsc[:, 0:1], col(C_FW), col(C_CP), None, ALU.mult).then_inc(w_scaled, 1)
            for k, (dst, src, scale) in enumerate(((wv_s, wv32, C_SW), (a_s, a32, C_SA))):
                dve.wait_ge(a_hi, k + 1)
                v.scalar_tensor_tensor(out=dst[:, LO], in0=src, scalar=col(scale), in1=dst[:, HI],
                                       op0=ALU.mult, op1=ALU.subtract).then_inc(weights_split, 1)
            base_links = links[0]

            def ln_variance(k, r):
                v.bn_aggr(mv[:, r], bn6[:, r]).then_inc(aggr_done, 1)
                dve.wait_ge(aggr_done, k + 1)
                v.tensor_scalar(var_s[:, r:r + 1], mv[:, r, 1:2], EPS, XN ** -2, ALU.add, ALU.mult).then_inc(ln_var, 1)

            def ln_rows(k, r, src, free):
                dve.wait_ge(ln_rstd, k + 1)
                if free:
                    dve.wait_ge(xn_lo, k - 1)
                v.tensor_scalar(xn32[:, r], src, mv[:, r, 0:1], rstd[:, r:r + 1], ALU.subtract,
                                ALU.mult).then_inc(xn_ready, 1)

            def ctx_scale(batch, par, nth):
                dve.wait_ge(ctx_max_all, batch + 1)

                def after(ins, n):
                    ins.then_inc(link, 1)
                    dve.wait_ge(link, nth * 4 + base_links + n)

                after(v.scalar_tensor_tensor(out=col(C_CM), in0=call[:, 0:1], scalar=TINY, in1=call[:, 1:2],
                                             op0=ALU.max, op1=ALU.max), 1)
                after(v.tensor_scalar(col(C_CP).bitcast(I32), col(C_CM).bitcast(I32), 0x7F800000, None,
                                      ALU.bitwise_and), 2)
                after(v.reciprocal(col(C_CR), col(C_CP)), 3)
                v.tensor_scalar(esc[:, par:par + 1], col(C_EA), col(C_CP), None, ALU.mult)
                v.tensor_scalar(fsc[:, par:par + 1], col(C_FW), col(C_CP), None, ALU.mult)
                after(v.tensor_scalar(csc[:, :], col(C_CR), TOP, None, ALU.mult), 4)
                v.tensor_copy(col(C_CR), csc[:, :]).then_inc(ctx_scaled, 1)

            def slot(it, s, last=False):
                t = it * BODY + s
                live = s >= 0 and (not last or t < NT)
                i, r = s % TB, s % 2
                if live:
                    dve.wait_ge(s_mm, t + 1)
                    diag = s_ps[:, i * P:(i + 1) * P]
                    v.tensor_tensor(diag, diag, causal[:, :], ALU.add).then_inc(s_masked, 1)
                    dve.wait_ge(s_masked, t + 1)
                    v.tensor_reduce(negmax[:, r:r + 1], s_ps[:, 0:(i + 1) * P], AX.X, ALU.max,
                                    negate=True).then_inc(s_max, 1)
                    dve.wait_ge(s_max, t + 1)
                    par = (s // TB) % 2
                    v.tensor_scalar(ebias[:, r:r + 1], negmax[:, r:r + 1], esc[:, par:par + 1], None,
                                    ALU.mult).then_inc(s_bias, 1)
                k, rk = t + LN_LEAD, (s + LN_LEAD) % 2
                norm = not last or k < NT + GT
                if norm:
                    if not last or k < NT:
                        src = x_ring[:, (s + LN_LEAD) % 8]
                        dve.wait_ge(x_in[(s + LN_LEAD) % 8], it * 2 * 16 + ((s + LN_LEAD) // 8 + 1) * 16)
                    else:
                        src = x2_in[:, k - NT]
                        dve.wait_ge(x2_loaded[k - NT], 16)
                    v.bn_stats(bn6[:, rk], src).then_inc(bn_done, 1)
                if s >= 1:
                    w = ((s - 1) % TB + 1) * P
                    if norm:
                        dve.wait_ge(bn_done, k + 1)
                    dve.wait_ge(p_tr, t)
                    v.tensor_copy(pT[:, :, 0:w], pT_ps[:, :, 0:w]).then_inc(pT_ready, 1)
                elif norm:
                    dve.wait_ge(bn_done, k + 1)
                if norm:
                    ln_variance(k, rk)
                if live:
                    dve.wait_ge(p_hi, t + 1)
                    v.scalar_tensor_tensor(out=p_s[:, LO, 0:(i + 1) * P], in0=p32[:, 0:(i + 1) * P], scalar=P_UP,
                                           in1=p_s[:, HI, 0:(i + 1) * P], op0=ALU.mult,
                                           op1=ALU.subtract).then_inc(p_split, 1)
                if s >= -T_LEAD and (not last or t < NT - T_LEAD):
                    pr, h = ((s + T_LEAD) // 2) % 2, s % 2
                    dve.wait_ge(t_hi, t + T_LEAD + 1)
                    v.scalar_tensor_tensor(out=tT[:, pr, LO, 2 * h:2 * h + 2], in0=t_ps[:, :, :], scalar=T_DOWN,
                                           in1=tT[:, pr, HI, 2 * h:2 * h + 2], op0=ALU.mult,
                                           op1=ALU.subtract).then_inc(t_split, 1)
                if norm:
                    ln_rows(k, rk, src, s + LN_LEAD >= 2)
                if s >= 1:
                    q = (s - 1) % 2
                    v.reciprocal(rinv[:, q:q + 1], rowsum[:, q:q + 1]).then_inc(o_inv, 1)
                    dve.wait_ge(o_inv, t)
                    par = ((s - 1) // TB) % 2
                    v.tensor_scalar(osc[:, q:q + 1], rinv[:, q:q + 1], fsc[:, par:par + 1], None,
                                    ALU.mult).then_inc(o_scaled, 1)
                    dve.wait_ge(o_scaled, t)
                    dve.wait_ge(pv_mm, t)
                    dve.wait_ge(x2_stored[(s - 1) % 4], it * (BODY // 4) * 16 + ((s - 1) // 4 + 1) * 16)
                    v.scalar_tensor_tensor(out=x2_ring[:, (s - 1) % 4], in0=o_ps[:, :], scalar=osc[:, q:q + 1],
                                           in1=x_ring[:, (s - 1) % 8], op0=ALU.mult, op1=ALU.add).then_inc(o_done, 1)
                if s >= -1 and (not last or t + 1 < NT):
                    j, par = (s + 1) % TB, ((s + 1) // TB) % 2
                    dve.wait_ge(v_hi, t + 2)
                    v.scalar_tensor_tensor(out=v_s[:, par, LO, j], in0=v_ps[:, :], scalar=V_DOWN,
                                           in1=v_s[:, par, HI, j], op0=ALU.mult,
                                           op1=ALU.subtract).then_inc(v_split, 1)
                if s > 0 and (not last or t + TB < NT):
                    batch, c = it * 2 + s // TB + 1, ctx_step(s)
                    if c in (1, 2):
                        half = slice((c - 1) * DC * S // 2, c * DC * S // 2)
                        if c == 1:
                            dve.wait_ge(ctx_in, batch * 16 + 16)
                        ins = v.tensor_reduce(cmax[:, c - 1:c], raw[:, half], AX.X, ALU.max,
                                              apply_absolute_value=True)
                        if c == 2:
                            ins.then_inc(ctx_max, 1)
                    if c == 4:
                        ctx_scale(batch, (s // TB + 1) % 2, batch - 1)
                    for q in CTX_SPLITS.get(c, ()):
                        ctx_lower(batch, (s // TB + 1) % 2, q)
                if last and t == TERN_SLOT - 1:
                    dve.wait_ge(w_summed, NW)
                    v.tensor_reduce(wtot[:, 0:2], wsum[:, :].rearrange("p (w n) -> p w n", w=2), AX.X,
                                    ALU.add).then_inc(w_total, 1)
                if last and TERN_SLOT <= t < TERN_SLOT + NW // 2:
                    if t == TERN_SLOT:
                        dve.wait_ge(w_total_all, 1)
                        for w, th, nth in ((0, C_TH1, C_NTH1), (1, C_TH2, C_NTH2)):
                            v.tensor_scalar(col(th), wtot[:, 2 + w:3 + w], 0.5 / (D * FC * P), 0.5e-8, ALU.mult,
                                            ALU.max).then_inc(w_thresh, 1)
                            dve.wait_ge(w_thresh, 2 * w + 1)
                            v.tensor_scalar(col(nth), col(th), -1.0, None, ALU.mult).then_inc(w_thresh, 1)
                            dve.wait_ge(w_thresh, 2 * w + 2)
                    for n in range(2 * (t - TERN_SLOT), 2 * (t - TERN_SLOT) + 2):
                        th, nth = ((C_TH1, C_NTH1), (C_TH2, C_NTH2))[n // (NW // 2)]
                        m = NW + n
                        dve.wait_ge(w_loaded[m % 2], 16 * (m // 2 + 1))
                        if n:
                            dve.wait_ge(w_ternary, n)
                        v.tensor_scalar(w_neg[:, :], w_in[:, m % 2], col(nth), None, ALU.is_lt).then_inc(w_negs, 1)
                        dve.wait_ge(w_negs, n + 1)
                        v.scalar_tensor_tensor(out=w_dst(n), in0=w_in[:, m % 2], scalar=col(th), in1=w_neg[:, :],
                                               op0=ALU.is_gt, op1=ALU.subtract).then_inc(w_ternary, 1)

            for s in range(FIRST_SLOT, 1):
                slot(0, s)
            with dve.Fori(0, TURNS - 1) as it:
                for s in range(1, BODY + 1):
                    slot(it, s)
            for s in range(1, BODY + 1):
                slot(TURNS - 1, s, last=True)

            def hidden(F, f, bn_tile=None):
                if bn_tile is not None:
                    dve.wait_ge(bn_done, bn_tile + 1)
                dve.wait_ge(g_hi, F + 1)
                v.scalar_tensor_tensor(out=g_s[:, f % 4, LO], in0=g32[:, f % 2], scalar=col(C_SG),
                                       in1=g_s[:, f % 4, HI], op0=ALU.mult, op1=ALU.subtract).then_inc(g_split, 1)

            def group(it, gg, last=False):
                g = it * 2 + gg
                for f in range(FC):
                    F = g * FC + f
                    norm = f in LN_STEPS and (not last or F + FC < NG * FC)
                    if norm:
                        i = LN_STEPS.index(f)
                        u = ((gg + 1) % 2) * GT + i
                        k = NT + GT + g * GT + i
                        dve.wait_ge(x2_loaded[u], (it * 16 + 16) if gg == 0 else (it * 16 + 32))
                        v.bn_stats(bn6[:, i % 2], x2_in[:, u]).then_inc(bn_done, 1)
                    if not last or F + 2 < NG * FC:
                        hidden(F + 2, f + 2, k if norm else None)
                    if norm:
                        ln_variance(k, i % 2)
                        ln_rows(k, i % 2, x2_in[:, u], True)
                    if f == FC - 1:
                        for i in range(GT):
                            dve.wait_ge(y_mm, g * GT + i + 1)
                            dve.wait_ge(x2_biased, g * GT + i + 1)
                            dve.wait_ge(y_stored[i], (g + 1) * 16)
                            v.scalar_tensor_tensor(out=y_out[:, i], in0=y_ps[i], scalar=col(C_FG),
                                                   in1=x2_in[:, gg * GT + i], op0=ALU.mult,
                                                   op1=ALU.add).then_inc(y_done, 1)

            hidden(0, 0)
            hidden(1, 1)
            with dve.Fori(0, NG // 2 - 1) as it:
                group(it, 0)
                group(it, 1)
            group(NG // 2 - 1, 0, last=True)
            group(NG // 2 - 1, 1, last=True)

        @block.tensor
        def _(pe):
            mm = nc.tensor.matmul

            pe.wait_ge(w_qk_in, 32)
            for m in range(DC):
                for c in range(DC):
                    last_mm = mm(a_ps[m], wqk_in[:, 0, c, m * P:(m + 1) * P], wqk_in[:, 1, c, :],
                                 start=(c == 0), stop=(c == DC - 1))
                last_mm.then_inc(a_mm, 1)
            pe.wait_ge(consts, 5)

            def transposes(k, r):
                pe.wait_ge(xn_lo, k + 1)
                if not isinstance(k, int) or k > 0:
                    pe.wait_ge(xT_ready, k)
                for a in (HI, LO):
                    for c in range(DC):
                        tr = nc.tensor.transpose(xT_ps[:, a, c], xn_s[:, r, a, c * P:(c + 1) * P], ident[:, :])
                tr.then_inc(x_tr, 1)

            def slot(it, s, last=False):
                t = it * BODY + s
                i = s % TB
                if s >= 0 and (not last or t < NT):
                    par, pr, q = (s // TB) % 2, (s // 2) % 2, s % 2
                    pe.wait_ge(t_split, t - q + 2)
                    pe.wait_ge(ctx_split, it * 8 + s // TB * 4 + i // 2 + 1)
                    if s >= 1:
                        pe.wait_ge(p_exp, t)
                    w = (i + 1) * P
                    for lo in range(0, w, 512):
                        hi = min(w, lo + 512)
                        for n, (ta, ca) in enumerate(PASSES):
                            for c in range(DC):
                                last_mm = mm(s_ps[:, lo:hi], tT[:, pr, ta, c, q * P:(q + 1) * P],
                                             ctx_s[:, par, ca, c, lo:hi], start=(n == 0 and c == 0),
                                             stop=(n == 2 and c == DC - 1))
                    last_mm.then_inc(s_mm, 1)
                if s >= 1:
                    pe.wait_ge(p_split, t)
                    for a in (HI, LO):
                        for j in range((s - 1) % TB + 1):
                            tr = nc.tensor.transpose(pT_ps[:, a, j * P:(j + 1) * P], p_s[:, a, j * P:(j + 1) * P],
                                                     ident[:, :])
                    tr.then_inc(p_tr, 1)
                if s >= -T_LEAD and (not last or t < NT - T_LEAD):
                    pr, h = ((s + T_LEAD) // 2) % 2, s % 2
                    pe.wait_ge(xT_ready, t + T_LEAD - h + 2)
                    if s == -T_LEAD:
                        pe.wait_ge(weights_split, 2)
                    else:
                        pe.wait_ge(t_split, t + T_LEAD)
                    for dd in range(2):
                        d = 2 * h + dd
                        for n, (xa, aa) in enumerate(PASSES):
                            for c in range(DC):
                                last_mm = mm(t_ps[:, dd], a_s[:, aa, c, d * P:(d + 1) * P], xnT[:, pr, xa, c, :],
                                             start=(n == 0 and c == 0), stop=(n == 2 and c == DC - 1))
                    last_mm.then_inc(t_mm, 1)
                if s >= 1:
                    pe.wait_ge(pT_ready, t)
                    pe.wait_ge(v_split, t + 1 if not last or t < NT else NT)
                    if last and t == NT:
                        pe.wait_ge(o_done, NT - 1)
                    jn, par = (s - 1) % TB, ((s - 1) // TB) % 2
                    for n, (pa, va) in enumerate(PASSES):
                        for j in range(jn + 1):
                            last_mm = mm(o_ps[:, :], pT[:, pa, j * P:(j + 1) * P], v_s[:, par, va, j],
                                         start=(n == 0 and j == 0), stop=(n == 2 and j == jn))
                    last_mm.then_inc(pv_mm, 1)
                if s >= -1 and (not last or t + 1 < NT):
                    j, par = (s + 1) % TB, ((s + 1) // TB) % 2
                    pe.wait_ge(ctx_split, it * 8 + (s + 1) // TB * 4 + j // 2 + 1)
                    if s >= 0:
                        pe.wait_ge(v_split, t + 1)
                    for n, (ca, va) in enumerate(PASSES):
                        for c in range(DC):
                            last_mm = mm(v_ps[:, :], ctx_s[:, par, ca, c, j * P:(j + 1) * P], wv_s[:, va, c, :],
                                         start=(n == 0 and c == 0), stop=(n == 2 and c == DC - 1))
                    last_mm.then_inc(v_mm, 1)
                if s >= -XT_LEAD and (not last or t + XT_LEAD < NT + GT):
                    transposes(t + XT_LEAD, (s + XT_LEAD) % 2)

            for s in range(FIRST_SLOT, 1):
                slot(0, s)
            with pe.Fori(0, TURNS - 1) as it:
                for s in range(1, BODY + 1):
                    slot(it, s)
            for s in range(1, BODY + 1):
                slot(TURNS - 1, s, last=True)

            def hidden(F, f, g):
                if f % FC == 0:
                    pe.wait_ge(xT_ready, NT + (g + 1) * GT)
                if f >= 2:
                    pe.wait_ge(g_act, F - 1)
                for a in (HI, LO):
                    for c in range(DC):
                        last_mm = mm(h_ps[f % 2], w1_s[:, c, (f % FC) * P:(f % FC + 1) * P],
                                     yT[:, (f // FC) % 2, a, c, :], start=(a == HI and c == 0),
                                     stop=(a == LO and c == DC - 1))
                last_mm.then_inc(h_mm, 1)

            def group(it, gg, last=False):
                g = it * 2 + gg
                for f in range(FC):
                    F = g * FC + f
                    if not last or F + 2 < NG * FC:
                        hidden(F + 2, gg * FC + f + 2, g + (f + 2) // FC)
                    pe.wait_ge(g_split, F + 1)
                    if f == 0:
                        pe.wait_ge(y_done, (g + 1) * GT)
                    for i in range(GT):
                        for a in (HI, LO):
                            last_mm = mm(y_ps[i], g_s[:, f % 4, a, i * P:(i + 1) * P], w2_s[:, f, :],
                                         start=(f == 0 and a == HI), stop=(f == FC - 1 and a == LO))
                        if f == FC - 1:
                            last_mm.then_inc(y_mm, 1)
                    if f in XT_STEPS and (not last or F + FC < NG * FC):
                        i = XT_STEPS.index(f)
                        transposes(NT + GT + g * GT + i, i % 2)

            pe.wait_ge(w_ternary, NW)
            pe.wait_ge(o_done, NT)
            hidden(0, 0, 0)
            hidden(1, 1, 0)
            with pe.Fori(0, NG // 2 - 1) as it:
                group(it, 0)
                group(it, 1)
            group(NG // 2 - 1, 0, last=True)
            group(NG // 2 - 1, 1, last=True)


def kernel(x, ctx_1024, g_xattn, g_ffn, L0_xattn_w_q, L0_xattn_w_k, L0_xattn_w_v, L0_ffn_W1, L0_ffn_b1,
           L0_ffn_W2, L0_ffn_b2):
    import numpy as np
    import concourse.bacc as bacc
    from concourse.bass_utils import run_bass_kernel_spmd

    B, S, D = x.shape
    C = D // P

    def chunks(a):
        return np.ascontiguousarray(a.reshape(a.shape[0] // P, P, -1).transpose(1, 0, 2))

    arrays = {
        "x": np.ascontiguousarray(np.asarray(x).reshape(B * S, D)),
        "ctxT": np.ascontiguousarray(np.asarray(ctx_1024).transpose(0, 2, 1).reshape(B, C, P, S).transpose(0, 2, 1, 3)),
        "g_xattn": np.asarray(g_xattn),
        "g_ffn": np.asarray(g_ffn),
        "wqT": chunks(np.asarray(L0_xattn_w_q).T),
        "wkT": chunks(np.asarray(L0_xattn_w_k).T),
        "wv": chunks(np.asarray(L0_xattn_w_v)),
        "w1T": chunks(np.asarray(L0_ffn_W1).T).reshape(P, -1),
        "b1c": np.ascontiguousarray(np.asarray(L0_ffn_b1).reshape(-1, P).T),
        "w2T": chunks(np.asarray(L0_ffn_W2).T).reshape(P, -1),
        "b2": np.asarray(L0_ffn_b2),
    }
    nc = bacc.Bacc("TRN2", target_bir_lowering=False, num_devices=1)
    args = {n: nc.dram_tensor(f"in_{n}", a.shape, mybir.dt.from_np(a.dtype), kind="ExternalInput").ap()
            for n, a in arrays.items()}
    out = nc.dram_tensor("out_y", (B * S, D), F32, kind="ExternalOutput").ap()
    gated_block(nc, *args.values(), out)
    r = run_bass_kernel_spmd(nc, [{f"in_{n}": a for n, a in arrays.items()}], core_ids=[0])
    return r.results[0]["out_y"].reshape(B, S, D)
```

```python
from contextlib import ExitStack
import math

import concourse.bass as bass
from concourse import mybir

ALU = mybir.AluOpType
ACT = mybir.ActivationFunctionType
AX = mybir.AxisListType
F32 = mybir.dt.float32
F16 = mybir.dt.float16
I32 = mybir.dt.int32
RMAX = bass.bass_isa.ReduceOp.max
RADD = bass.bass_isa.ReduceOp.add

P = 128
HI, LO = 0, 1
PASSES = ((HI, HI), (LO, HI), (HI, LO))


def gated_block(nc, x, ctxT, g_xattn, g_ffn, wqT, wkT, wv, w1T, b1c, w2T, b2, out):
    B, _, DC, S = ctxT.shape
    N, D = x.shape
    FC = b1c.shape[1]
    NT = N // P
    TB = S // P
    BODY = 2 * TB
    TURNS = NT // BODY
    GT = 4
    NG = NT // GT
    EPS = 1e-5
    NEG = -3.0e38

    XN = 2.0 ** 10
    TOP = 2.0 ** 13
    T_DOWN = 2.0 ** -18
    V_DOWN = 2.0 ** -22
    P_UP = 2.0 ** 14
    G_TOP = 2.0 ** 14
    TINY = 2.0 ** -40

    x_tiles = x.rearrange("(t p) d -> t p d", p=P)
    out_tiles = out.rearrange("(t p) d -> t p d", p=P)

    es = ExitStack()
    with es:
        def sb(name, shape, dt=F32):
            return es.enter_context(nc.sbuf_tensor(name, shape, dt))

        def ps(name, shape, dt=F32):
            return es.enter_context(nc.psum_tensor(name, shape, dt))

        def sem(name):
            return es.enter_context(nc.semaphore(name))

        a_s = sb("a_s", [P, 2, DC, D], F16)
        wv_s = sb("wv_s", [P, 2, DC, D], F16)
        raw = sb("raw", [P, DC * S])
        ctx_s = sb("ctx_s", [P, 2, 2, DC, S], F16)
        tT = sb("tT", [P, 2, 2, DC, 2 * P], F16)
        v_s = sb("v_s", [P, 2, 2, TB, D], F16)
        xnT = sb("xnT", [P, 2, 2, DC, 2 * P], F16)
        x_ring = sb("x_ring", [P, 8, D])
        xn32 = sb("xn32", [P, 2, D])
        xn_s = sb("xn_s", [P, 2, 2, D], F16)
        p32 = sb("p32", [P, S])
        p_s = sb("p_s", [P, 2, S], F16)
        pT = sb("pT", [P, 2, S], F16)
        x2_ring = sb("x2_ring", [P, 4, D])
        w1_s = sb("w1_s", [P, DC, FC * P], F16)
        w2_s = sb("w2_s", [P, FC, D], F16)
        WR = 3
        WCH = 1024
        w_in = sb("w_in", [P, WR, WCH])
        g32 = sb("g32", [P, 2, 4 * P])
        w_neg = g32[:, 1].bitcast(F16)
        b2_row = sb("b2_row", [P, D])
        b1_s = sb("b1_s", [P, FC])
        ident = sb("ident", [P, P], F16)
        causal = sb("causal", [P, P])
        bn6 = sb("bn6", [P, 2, 6])
        mv = sb("mv", [P, 2, 2])
        var_s = sb("var_s", [P, 2])
        rstd = sb("rstd", [P, 2])
        minus_half = sb("minus_half", [P, 1])
        negmax = sb("negmax", [P, 2])
        ebias = sb("ebias", [P, 2])
        rowsum = sb("rowsum", [P, 2])
        rinv = sb("rinv", [P, 2])
        osc = sb("osc", [P, 2])
        cmax = sb("cmax", [P, 2])
        call = sb("call", [P, 2])
        sc = sb("sc", [P, 40])
        esc = sb("esc", [P, 2])
        fsc = sb("fsc", [P, 2])
        csc = sb("csc", [P, 1])
        wsum = sb("wsum", [P, 16])
        wtot = sb("wtot", [P, 4])

        wqk_in = ctx_s[:, 1, :, :, :].rearrange("p a c s -> p (a c s)").bitcast(F32) \
            .rearrange("p (w c d) -> p w c d", w=2, c=DC)
        prod_in = v_s[:, 1, :, :, :].rearrange("p a t d -> p (a t d)").bitcast(F32) \
            .rearrange("p (w c d) -> p w c d", w=2, c=DC)
        wv32 = prod_in[:, 0]

        x2_in = raw[:, :].rearrange("p (t d) -> p t d", d=D)
        yT = ctx_s[:, 0, :, :, :].rearrange("p a c s -> p (a c s)") \
            .rearrange("p (g a c n) -> p g a c n", g=2, a=2, c=DC)
        v_old = v_s[:, 0, :, :, :].rearrange("p a t d -> p (a t d)")
        g_s = v_old[:, 0:4 * 2 * 512].rearrange("p (r a n) -> p r a n", r=4, a=2)
        y_out = v_old[:, 4096:8192].bitcast(F32).rearrange("p (t d) -> p t d", d=D)

        s_ps = ps("s_ps", [P, S])
        pT_ps = ps("pT_ps", [P, 2, S], F16)
        v_ps = ps("v_ps", [P, D])
        t_ps = ps("t_ps", [P, 2, 2 * P])
        o_ps = ps("o_ps", [P, D])
        xT_ps = ps("xT_ps", [P, 2, DC, P], F16)
        pT32 = pT_ps[:, :, :].rearrange("p a n -> p (a n)").bitcast(F32)
        a_ps = y_ps = [s_ps[:, 0:D], s_ps[:, D:2 * D], pT32[:, 0:D], pT32[:, D:2 * D]]
        h_ps = [v_ps[:, :], t_ps[:, :, :].rearrange("p a n -> p (a n)")]

        x_in = [sem(f"x_in{i}") for i in range(8)]
        ctx_in = sem("ctx_in")
        w_qk_in = [sem(f"w_qk_in{c}") for c in range(DC)]
        w_v_in, small_in = sem("w_v_in"), sem("small_in")
        consts = sem("consts")
        a_mm, amax, amax_all = sem("a_mm"), sem("amax"), sem("amax_all")
        wmax, wmax_all = sem("wmax"), sem("wmax_all")
        link = sem("link")
        wv_scaled, wv_hi, wv_split = sem("wv_scaled"), sem("wv_hi"), sem("wv_split")
        a_scaled, a_hi, a_split = sem("a_scaled"), sem("a_hi"), sem("a_split")
        tanh_done = sem("tanh_done")
        ctx_max, ctx_max_all, ctx_scaled = sem("ctx_max"), sem("ctx_max_all"), sem("ctx_scaled")
        ctx_hi, ctx_split = sem("ctx_hi"), sem("ctx_split")
        bn_done, aggr_done, ln_var, ln_rstd = sem("bn_done"), sem("aggr_done"), sem("ln_var"), sem("ln_rstd")
        xn_ready, xn_hi, xn_lo = sem("xn_ready"), sem("xn_hi"), sem("xn_lo")
        x_tr, xT_ready = sem("x_tr"), sem("xT_ready")
        t_mm, t_hi, t_split = sem("t_mm"), sem("t_hi"), sem("t_split")
        v_mm, v_hi, v_split = sem("v_mm"), sem("v_hi"), sem("v_split")
        s_mm, s_masked, s_max, s_bias = sem("s_mm"), sem("s_masked"), sem("s_max"), sem("s_bias")
        p_exp, p_hi, p_split = sem("p_exp"), sem("p_hi"), sem("p_split")
        p_tr, pT_ready = sem("p_tr"), sem("pT_ready")
        pv_mm, o_inv, o_scaled, o_done = sem("pv_mm"), sem("o_inv"), sem("o_scaled"), sem("o_done")
        x2_stored = [sem(f"x2_stored{i}") for i in range(4)]
        w_loaded = [sem(f"w_loaded{i}") for i in range(WR)]
        w_summed, w_total, w_total_all, w_thresh = sem("w_summed"), sem("w_total"), sem("w_total_all"), sem("w_thresh")
        w_negs, w_ternary = sem("w_negs"), sem("w_ternary")
        x2_loaded = [sem(f"x2_loaded{i}") for i in range(8)]
        x2_biased = sem("x2_biased")
        h_mm, g_act, g_hi, g_split = sem("h_mm"), sem("g_act"), sem("g_hi"), sem("g_split")
        y_mm, y_done = sem("y_mm"), sem("y_done")
        y_stored = [sem(f"y_stored{i}") for i in range(4)]

        (C_TANH0, C_TANH1, C_G0, C_G1, C_WMAX, C_BMAX, C_MA, C_PA, C_PW, C_PG, C_SA, C_SW, C_SG,
         C_EA, C_FW, C_FG, C_TH1, C_NTH1, C_TH2, C_NTH2, C_CM, C_CP, C_CR, C_ALLA) = range(24)

        def col(c, n=1):
            return sc[:, c:c + n]

        C_ALLW, C_AMAX = C_ALLA + 2, C_ALLA + 4
        PRODUCTS = {-5: (0, 1), -4: (2,), -3: (3,)}
        A_SLOT, C_SLOT = -3, -2

        ctx_batches = ctxT
        LN_LEAD, XT_LEAD, T_LEAD = 5, 4, 2
        FIRST_SLOT = -LN_LEAD
        W_PLAN = {NT - 15: "SSS", NT - 14: "SSS", NT - 13: "SSS", NT - 12: "SS", NT - 11: "TS", NT - 10: "TS",
                  NT - 9: "TS", NT - 8: "TS", NT - 7: "TS", NT - 6: "TT", NT - 5: "TT", NT - 4: "TT", NT - 3: "TT",
                  NT - 2: "TT", NT - 1: "T"}
        TOTAL_SLOTS = {NT - 12: 0, NT - 6: 1}
        FIRST_SPLITS = {-2: (0,), -1: (1, 2), 0: (3,)}
        CTX_SPLITS = {5: (0,), 6: (1, 2), 7: (3,)}

        def ctx_step(s):
            return s % TB

        W_CHUNKS = [(src, dst, k) for src, dst in ((w1T, w1_s), (w2T, w2_s)) for k in range(DC * FC * P // WCH)]
        NW = len(W_CHUNKS)

        W_STEPS = []
        for at, kinds in W_PLAN.items():
            for kind in kinds:
                W_STEPS.append((at, kind, sum(k == kind for _, k, _ in W_STEPS)))

        def w_turn(t, kind):
            return [(m, n) for m, (at, k, n) in enumerate(W_STEPS) if at == t and k == kind]

        def w_dst(n):
            _, dst, k = W_CHUNKS[n]
            return dst[:, :, :].rearrange("p a n -> p (a n)")[:, k * WCH:(k + 1) * WCH]

        LN_STEPS = (2, 4, 7, 10)
        XT_STEPS = (4, 6, 9, 12)

        block = es.enter_context(nc.Block())

        @block.sync
        def _(sp):
            def load_x(tile):
                sp.dma_start(x_ring[:, tile], x_tiles[tile]).then_inc(x_in[tile], 16)

            load_x(0)
            for c in range(DC):
                sp.dma_start(wqk_in[:, 0, c], wqT[:, c]).then_inc(w_qk_in[c], 16)
                sp.dma_start(wqk_in[:, 1, c], wkT[:, c]).then_inc(w_qk_in[c], 16)
                if c < 2:
                    load_x(c + 1)
            sp.dma_start(wv32, wv).then_inc(w_v_in, 16)
            sp.dma_start(raw[:, :], ctx_batches[0].rearrange("p c s -> p (c s)")).then_inc(ctx_in, 16)
            for t in range(3, 8):
                load_x(t)

            def load_ctx(batch):
                sp.wait_ge(ctx_split, 4 * batch)
                sp.dma_start(raw[:, :], ctx_batches[batch].rearrange("p c s -> p (c s)")).then_inc(ctx_in, 16)

            def load_weights(m):
                if m >= WR:
                    _, kind, n = W_STEPS[m - WR]
                    sp.wait_ge(w_summed if kind == "S" else w_ternary, n + 1)
                src, _, k = W_CHUNKS[W_STEPS[m][2]]
                sp.dma_start(w_in[:, m % WR], src[:, k * WCH:(k + 1) * WCH]).then_inc(w_loaded[m % WR], 16)

            def load_x2(tile, u):
                sp.dma_start(x2_in[:, u], out_tiles[tile]).then_inc(x2_loaded[u], 16)

            def slot(it, s, last=False):
                t = it * BODY + s
                if last:
                    for m, (at, _, _) in enumerate(W_STEPS):
                        if at == t:
                            load_weights(m)
                if not last or t + 7 < NT:
                    sp.wait_ge(o_done, t)
                    sp.dma_start(x_ring[:, (s + 7) % 8], x_tiles[t + 7]).then_inc(x_in[(s + 7) % 8], 16)
                sp.wait_ge(o_done, t)
                sp.dma_start(out_tiles[t - 1], x2_ring[:, (s - 1) % 4]).then_inc(x2_stored[(s - 1) % 4], 16)
                if s % TB == 7 and (not last or t + 9 < NT):
                    load_ctx(it * 2 + s // TB + 2)

            for i in range(4):
                sp.sem_inc(x2_stored[i], 16)
                sp.sem_inc(y_stored[i], 16)
            sp.sem_inc(y_done, GT)
            load_ctx(1)
            with sp.Fori(0, TURNS - 1) as it:
                for s in range(1, BODY + 1):
                    slot(it, s)
            for s in range(1, BODY + 1):
                slot(TURNS - 1, s, last=True)
                if s == BODY - 6:
                    sp.wait_ge(ctx_split, 4 * B)
                    for i in range(4):
                        sp.wait_ge(x2_stored[i], 2 * 16)
                        load_x2(i, i)
            for i in range(4):
                sp.wait_ge(x2_stored[i], 16 * (NT // 4 + 1))

            def group(it, gg, last=False):
                g = it * 2 + gg
                if not last or g + 1 < NG:
                    sp.wait_ge(y_done, (g + 1) * GT)
                    for i in range(GT):
                        load_x2(g * GT + GT + i, ((gg + 1) % 2) * GT + i)
                for i in range(GT):
                    sp.wait_ge(y_done, (g + 1) * GT + i + 1)
                    sp.dma_start(out_tiles[g * GT + i], y_out[:, i]).then_inc(y_stored[i], 16)

            with sp.Fori(0, NG // 2 - 1) as it:
                group(it, 0)
                group(it, 1)
            group(NG // 2 - 1, 0, last=True)
            group(NG // 2 - 1, 1, last=True)
            for i in range(4):
                sp.wait_ge(y_stored[i], 16 * (NG + 1))

        @block.gpsimd
        def _(pool):
            g = nc.gpsimd
            g.memset(ident[:, :], 0.0).then_inc(consts, 1)
            g.memset(causal[:, :], 0.0).then_inc(consts, 1)
            g.memset(minus_half[:, :], -0.5).then_inc(consts, 1)
            pool.wait_ge(consts, 3)
            g.affine_select(out=ident[:, :], in_=ident[:, :], compare_op=ALU.not_equal, fill=1.0, base=0,
                            pattern=[[-1, P]], channel_multiplier=1).then_inc(consts, 1)
            g.affine_select(out=causal[:, :], in_=causal[:, :], compare_op=ALU.is_ge, fill=NEG, base=0,
                            pattern=[[-1, P]], channel_multiplier=1).then_inc(consts, 1)
            pool.wait_ge(small_in, 64)

            def norm(it, s, ctx_batch=None):
                k = it * BODY + s + LN_LEAD
                r = (s + LN_LEAD) % 2
                pool.wait_ge(ln_var, k + 1)
                g.tensor_tensor(rstd[:, r:r + 1], var_s[:, r:r + 1], minus_half[:, :], ALU.pow).then_inc(ln_rstd, 1)
                pool.wait_ge(xn_hi, k + 1)
                if ctx_batch is not None:
                    pool.wait_ge(ctx_max, ctx_batch + 1)
                if s + LN_LEAD >= 2:
                    pool.wait_ge(x_tr, k - 1)
                g.tensor_tensor(xn_s[:, r, LO], xn32[:, r], xn_s[:, r, HI], ALU.subtract).then_inc(xn_lo, 1)

            def slot(it, s, last=False):
                t = it * BODY + s
                reduce_ctx = s > 0 and ctx_step(s) == 3 and (not last or t + TB < NT)
                if not last or t + LN_LEAD < NT + GT:
                    norm(it, s, it * 2 + s // TB + 1 if reduce_ctx else None)
                if last and t + LN_LEAD >= NT and t + LN_LEAD < NT + GT:
                    add_bias(t + LN_LEAD - NT, t + LN_LEAD - NT)
                if reduce_ctx:
                    g.partition_all_reduce(call[:, :], cmax[:, :], P, RMAX).then_inc(ctx_max_all, 1)
                if last and t in TOTAL_SLOTS:
                    w = TOTAL_SLOTS[t]
                    pool.wait_ge(w_total, w + 1)
                    g.partition_all_reduce(wtot[:, 2 + w:3 + w], wtot[:, w:w + 1], P, RADD).then_inc(w_total_all, 1)

            def add_bias(tile, u):
                pool.wait_ge(xn_ready, NT + tile + 1)
                g.tensor_tensor(x2_in[:, u], x2_in[:, u], b2_row[:, :], ALU.add).then_inc(x2_biased, 1)

            for s in range(FIRST_SLOT, 1):
                slot(0, s)
                if s == C_SLOT:
                    pool.wait_ge(ctx_max, 1)
                    g.partition_all_reduce(call[:, :], cmax[:, :], P, RMAX).then_inc(ctx_max_all, 1)
                if s == A_SLOT:
                    pool.wait_ge(wmax, 2)
                    g.partition_all_reduce(sc[:, C_ALLW:C_ALLW + 2], sc[:, C_WMAX:C_WMAX + 2], P,
                                           RMAX).then_inc(wmax_all, 1)
                    pool.wait_ge(amax, 1)
                    g.partition_all_reduce(sc[:, C_ALLA:C_ALLA + 2], sc[:, C_AMAX:C_AMAX + 2], P,
                                           RMAX).then_inc(amax_all, 1)
            with pool.Fori(0, TURNS - 1) as it:
                for s in range(1, BODY + 1):
                    slot(it, s)
            for s in range(1, BODY + 1):
                slot(TURNS - 1, s, last=True)

            def group(it, gg):
                for i in range(GT):
                    tile = it * 2 * GT + gg * GT + GT + i
                    r = i % 2
                    pool.wait_ge(ln_var, NT + tile + 1)
                    g.tensor_tensor(rstd[:, r:r + 1], var_s[:, r:r + 1], minus_half[:, :], ALU.pow).then_inc(ln_rstd, 1)
                    pool.wait_ge(xn_hi, NT + tile + 1)
                    pool.wait_ge(x_tr, NT + tile - 1)
                    g.tensor_tensor(xn_s[:, r, LO], xn32[:, r], xn_s[:, r, HI], ALU.subtract).then_inc(xn_lo, 1)
                    add_bias(tile, ((gg + 1) % 2) * GT + i)

            with pool.Fori(0, NG // 2 - 1) as it:
                group(it, 0)
                group(it, 1)
            group(NG // 2 - 1, 0)

        @block.scalar
        def _(act):
            a = nc.scalar
            act.dma_start(col(C_G0), g_xattn.partition_broadcast(P)).then_inc(small_in, 16)
            act.dma_start(col(C_G1), g_ffn.partition_broadcast(P)).then_inc(small_in, 16)
            act.dma_start(b1_s[:, :], b1c).then_inc(small_in, 16)
            act.dma_start(b2_row[:, :], b2.partition_broadcast(P)).then_inc(small_in, 16)
            act.wait_ge(small_in, 64)
            a.activation(col(C_TANH0, 2), col(C_G0, 2), ACT.Tanh).then_inc(tanh_done, 1)
            raw4 = raw[:, :].rearrange("p (c s) -> p c s", c=DC)

            def ctx_upper(batch, par, q):
                act.wait_ge(ctx_scaled, batch + 1)
                cols = slice(q * 2 * P, (q + 1) * 2 * P)
                a.activation(ctx_s[:, par, HI, :, cols], raw4[:, :, cols], ACT.Copy,
                             scale=csc[:, :]).then_inc(ctx_hi, 1)

            def softmax(it, s):
                t = it * BODY + s
                w = (s % TB + 1) * P
                r = s % 2
                act.wait_ge(s_bias, t + 1)
                act.wait_ge(p_split, t)
                a.activation(p32[:, 0:w], s_ps[:, 0:w], ACT.Exp, bias=ebias[:, r:r + 1],
                             scale=esc[:, (s // TB) % 2:(s // TB) % 2 + 1],
                             accum_out=rowsum[:, r:r + 1]).then_inc(p_exp, 1)
                act.wait_ge(p_exp, t + 1)
                act.wait_ge(p_tr, t)
                a.activation(p_s[:, HI, 0:w], p32[:, 0:w], ACT.Copy, scale=P_UP).then_inc(p_hi, 1)

            def sum_weight(m, n):
                act.wait_ge(w_loaded[m % WR], 16 * (m // WR + 1))
                a.activation(w_dst(n), w_in[:, m % WR], ACT.Abs, accum_out=wsum[:, n:n + 1]).then_inc(w_summed, 1)

            def slot(it, s, last=False):
                t = it * BODY + s
                if s >= 0 and (not last or t < NT):
                    softmax(it, s)
                if s >= -T_LEAD and (not last or t < NT - T_LEAD):
                    pr, h = ((s + T_LEAD) // 2) % 2, s % 2
                    act.wait_ge(t_mm, t + T_LEAD + 1)
                    a.activation(tT[:, pr, HI, 2 * h:2 * h + 2], t_ps[:, :, :], ACT.Copy,
                                 scale=T_DOWN).then_inc(t_hi, 1)
                if not last or t + LN_LEAD < NT + GT:
                    k = t + LN_LEAD
                    r = (s + LN_LEAD) % 2
                    act.wait_ge(xn_ready, k + 1)
                    if s + LN_LEAD >= 2:
                        act.wait_ge(x_tr, k - 1)
                    a.activation(xn_s[:, r, HI], xn32[:, r], ACT.Copy).then_inc(xn_hi, 1)
                if s > 0 and (not last or t + TB < NT):
                    for q in CTX_SPLITS.get(ctx_step(s), ()):
                        ctx_upper(it * 2 + s // TB + 1, (s // TB + 1) % 2, q)
                if s >= -1 and (not last or t + 1 < NT):
                    j, par = (s + 1) % TB, ((s + 1) // TB) % 2
                    act.wait_ge(v_mm, t + 2)
                    a.activation(v_s[:, par, HI, j], v_ps[:, :], ACT.Copy, scale=V_DOWN).then_inc(v_hi, 1)
                if s >= -XT_LEAD and (not last or t + XT_LEAD < NT + GT):
                    k = t + XT_LEAD
                    act.wait_ge(x_tr, k + 1)
                    if not last or k < NT:
                        pr, q = ((s + XT_LEAD) // 2) % 2, (s + XT_LEAD) % 2
                        dst = xnT[:, pr, :, :, q * P:(q + 1) * P]
                    else:
                        dst = yT[:, 0, :, :, (k - NT) * P:(k - NT + 1) * P]
                    a.activation(dst, xT_ps[:, :, :, :], ACT.Copy).then_inc(xT_ready, 1)
                for m, n in w_turn(t, "S") if last else ():
                    sum_weight(m, n)

            for s in range(FIRST_SLOT, 1):
                slot(0, s)
                if s == A_SLOT:
                    act.wait_ge(wv_scaled, 1)
                    a.activation(wv_s[:, HI], wv32, ACT.Copy, scale=col(C_SW)).then_inc(wv_hi, 1)
                    act.wait_ge(a_scaled, 1)
                    for m in range(DC):
                        a.activation(a_s[:, HI, m], a_ps[m], ACT.Copy, scale=col(C_SA)).then_inc(a_hi, 1)
                for q in FIRST_SPLITS.get(s, ()):
                    ctx_upper(0, 0, q)
            with act.Fori(0, TURNS - 1) as it:
                for s in range(1, BODY + 1):
                    slot(it, s)
            for s in range(1, BODY + 1):
                slot(TURNS - 1, s, last=True)

            def hidden(F, f):
                act.wait_ge(h_mm, F + 1)
                if f >= 2:
                    act.wait_ge(g_split, F - 1)
                a.activation(g32[:, f % 2], h_ps[f % 2], ACT.Gelu, bias=b1_s[:, f % FC:f % FC + 1],
                             scale=1.0 / XN).then_inc(g_act, 1)
                act.wait_ge(g_act, F + 1)
                a.activation(g_s[:, f % 4, HI], g32[:, f % 2], ACT.Copy, scale=col(C_SG)).then_inc(g_hi, 1)

            def group(it, gg, last=False):
                for f in range(FC):
                    F = it * 2 * FC + gg * FC + f
                    if not last or F + 2 < NG * FC:
                        hidden(F + 2, f + 2)
                    if f in LN_STEPS and (not last or F + FC < NG * FC):
                        i = LN_STEPS.index(f)
                        k = NT + GT + (it * 2 + gg) * GT + i
                        act.wait_ge(xn_ready, k + 1)
                        act.wait_ge(x_tr, k - 1)
                        a.activation(xn_s[:, i % 2, HI], xn32[:, i % 2], ACT.Copy).then_inc(xn_hi, 1)
                    if f in XT_STEPS and (not last or F + FC < NG * FC):
                        i = XT_STEPS.index(f)
                        k = NT + GT + (it * 2 + gg) * GT + i
                        act.wait_ge(x_tr, k + 1)
                        a.activation(yT[:, (gg + 1) % 2, :, :, i * P:(i + 1) * P], xT_ps[:, :, :, :],
                                     ACT.Copy).then_inc(xT_ready, 1)

            hidden(0, 0)
            hidden(1, 1)
            with act.Fori(0, NG // 2 - 1) as it:
                group(it, 0)
                group(it, 1)
            group(NG // 2 - 1, 0, last=True)
            group(NG // 2 - 1, 1, last=True)

        @block.vector
        def _(dve):
            v = nc.vector
            links = [0]

            def linked(ins):
                links[0] += 1
                ins.then_inc(link, 1)
                dve.wait_ge(link, links[0])

            def power_scale(mx, pw, scale, top):
                linked(v.tensor_scalar(mx, mx, TINY, None, ALU.max))
                linked(v.tensor_scalar(pw.bitcast(I32), mx.bitcast(I32), 0x7F800000, None, ALU.bitwise_and))
                linked(v.reciprocal(scale, pw))
                linked(v.tensor_scalar(scale, scale, top, None, ALU.mult))

            raw4 = raw[:, :].rearrange("p (c s) -> p c s", c=DC)

            def ctx_lower(batch, par, q):
                dve.wait_ge(ctx_hi, 4 * batch + q + 1)
                cols = slice(q * 2 * P, (q + 1) * 2 * P)
                v.scalar_tensor_tensor(out=ctx_s[:, par, LO, :, cols], in0=raw4[:, :, cols], scalar=csc[:, :],
                                       in1=ctx_s[:, par, HI, :, cols], op0=ALU.mult,
                                       op1=ALU.subtract).then_inc(ctx_split, 1)

            def scale_wv():
                dve.wait_ge(w_v_in, 16)
                v.tensor_reduce(col(C_WMAX), wv32, AX.XY, ALU.max, apply_absolute_value=True).then_inc(wmax, 1)
                dve.wait_ge(small_in, 64)
                v.tensor_reduce(col(C_BMAX), b1_s[:, :], AX.X, ALU.max, apply_absolute_value=True).then_inc(wmax, 1)
                dve.wait_ge(wmax_all, 1)
                linked(v.tensor_scalar(col(C_ALLW + 1), col(C_ALLW + 1), float(D), None, ALU.add))
                power_scale(col(C_ALLW, 2), col(C_PW, 2), col(C_SW, 2), TOP)
                v.tensor_scalar(col(C_SG), col(C_SG), G_TOP / TOP, None, ALU.mult).then_inc(wv_scaled, 1)
                dve.wait_ge(tanh_done, 1)
                linked(v.tensor_scalar(col(C_FW), col(C_PW), col(C_TANH0), 1.0 / (P_UP * V_DOWN * TOP * TOP),
                                       ALU.mult, ALU.mult))
                linked(v.tensor_scalar(col(C_FG), col(C_PG), col(C_TANH1), 1.0 / G_TOP, ALU.mult, ALU.mult))
                linked(v.tensor_scalar(b2_row[:, :], b2_row[:, :], col(C_TANH1), None, ALU.mult))

            def wv_lower():
                dve.wait_ge(wv_hi, 1)
                v.scalar_tensor_tensor(out=wv_s[:, LO], in0=wv32, scalar=col(C_SW), in1=wv_s[:, HI],
                                       op0=ALU.mult, op1=ALU.subtract).then_inc(wv_split, 1)

            def ctx_half(h):
                return v.tensor_reduce(cmax[:, h:h + 1], raw[:, h * DC * S // 2:(h + 1) * DC * S // 2], AX.X, ALU.max,
                                       apply_absolute_value=True)

            def scale_first_ctx():
                dve.wait_ge(ctx_max_all, 1)
                linked(v.tensor_tensor(col(C_CM), call[:, 0:1], call[:, 1:2], ALU.max))
                power_scale(col(C_CM), col(C_CP), col(C_CR), TOP)
                v.tensor_copy(csc[:, :], col(C_CR)).then_inc(ctx_scaled, 1)
                dve.wait_ge(ctx_scaled, 1)
                linked(v.tensor_scalar(fsc[:, 0:1], col(C_FW), col(C_CP), None, ALU.mult))
                linked(v.tensor_scalar(esc[:, 0:1], col(C_EA), col(C_CP), None, ALU.mult))

            def scale_product():
                for n, half in enumerate((s_ps[:, :], pT32)):
                    dve.wait_ge(a_mm, n + 1)
                    ins = v.tensor_reduce(col(C_AMAX + n), half, AX.X, ALU.max, apply_absolute_value=True)
                ins.then_inc(amax, 1)
                dve.wait_ge(amax_all, 1)
                linked(v.tensor_tensor(col(C_MA), col(C_ALLA), col(C_ALLA + 1), ALU.max))
                power_scale(col(C_MA), col(C_PA), col(C_SA), TOP)
                v.tensor_scalar(col(C_EA), col(C_PA), 1.0 / (XN * T_DOWN * TOP * TOP * math.sqrt(D)), None,
                                ALU.mult).then_inc(a_scaled, 1)
                for m in range(DC):
                    dve.wait_ge(a_hi, m + 1)
                    v.scalar_tensor_tensor(out=a_s[:, LO, m], in0=a_ps[m], scalar=col(C_SA), in1=a_s[:, HI, m],
                                           op0=ALU.mult, op1=ALU.subtract).then_inc(a_split, 1)

            def ln_variance(k, r):
                v.bn_aggr(mv[:, r], bn6[:, r]).then_inc(aggr_done, 1)
                dve.wait_ge(aggr_done, k + 1)
                v.tensor_scalar(var_s[:, r:r + 1], mv[:, r, 1:2], EPS, XN ** -2, ALU.add, ALU.mult).then_inc(ln_var, 1)

            def ln_rows(k, r, src, free):
                dve.wait_ge(ln_rstd, k + 1)
                if free:
                    dve.wait_ge(xn_lo, k - 1)
                v.tensor_scalar(xn32[:, r], src, mv[:, r, 0:1], rstd[:, r:r + 1], ALU.subtract,
                                ALU.mult).then_inc(xn_ready, 1)

            def ctx_scale(batch, par, nth):
                dve.wait_ge(ctx_max_all, batch + 1)

                def after(ins, n):
                    ins.then_inc(link, 1)
                    dve.wait_ge(link, nth * 4 + links[0] + n)

                after(v.scalar_tensor_tensor(out=col(C_CM), in0=call[:, 0:1], scalar=TINY, in1=call[:, 1:2],
                                             op0=ALU.max, op1=ALU.max), 1)
                after(v.tensor_scalar(col(C_CP).bitcast(I32), col(C_CM).bitcast(I32), 0x7F800000, None,
                                      ALU.bitwise_and), 2)
                after(v.reciprocal(col(C_CR), col(C_CP)), 3)
                v.tensor_scalar(esc[:, par:par + 1], col(C_EA), col(C_CP), None, ALU.mult)
                v.tensor_scalar(fsc[:, par:par + 1], col(C_FW), col(C_CP), None, ALU.mult)
                after(v.tensor_scalar(csc[:, :], col(C_CR), TOP, None, ALU.mult), 4)
                v.tensor_copy(col(C_CR), csc[:, :]).then_inc(ctx_scaled, 1)

            def slot(it, s, last=False):
                t = it * BODY + s
                live = s >= 0 and (not last or t < NT)
                i, r = s % TB, s % 2
                terns = w_turn(t, "T") if last else []
                k, rk = t + LN_LEAD, (s + LN_LEAD) % 2
                norm = not last or k < NT + GT
                if norm:
                    if not last or k < NT:
                        src = x_ring[:, (s + LN_LEAD) % 8]
                        dve.wait_ge(x_in[(s + LN_LEAD) % 8], it * 2 * 16 + ((s + LN_LEAD) // 8 + 1) * 16)
                    else:
                        src = x2_in[:, k - NT]
                        dve.wait_ge(x2_loaded[k - NT], 16)
                if s >= 1:
                    w = ((s - 1) % TB + 1) * P
                    dve.wait_ge(p_tr, t)
                    v.tensor_copy(pT[:, :, 0:w], pT_ps[:, :, 0:w]).then_inc(pT_ready, 1)
                if norm:
                    v.bn_stats(bn6[:, rk], src).then_inc(bn_done, 1)
                if live:
                    dve.wait_ge(s_mm, t + 1)
                    diag = s_ps[:, i * P:(i + 1) * P]
                    v.tensor_tensor(diag, diag, causal[:, :], ALU.add).then_inc(s_masked, 1)
                    dve.wait_ge(s_masked, t + 1)
                    v.tensor_reduce(negmax[:, r:r + 1], s_ps[:, 0:(i + 1) * P], AX.X, ALU.max,
                                    negate=True).then_inc(s_max, 1)
                    dve.wait_ge(s_max, t + 1)
                    if norm:
                        dve.wait_ge(bn_done, k + 1)
                    par = (s // TB) % 2
                    v.tensor_scalar(ebias[:, r:r + 1], negmax[:, r:r + 1], esc[:, par:par + 1], None,
                                    ALU.mult).then_inc(s_bias, 1)
                elif norm:
                    dve.wait_ge(bn_done, k + 1)
                if norm:
                    ln_variance(k, rk)
                if live:
                    dve.wait_ge(p_hi, t + 1)
                    v.scalar_tensor_tensor(out=p_s[:, LO, 0:(i + 1) * P], in0=p32[:, 0:(i + 1) * P], scalar=P_UP,
                                           in1=p_s[:, HI, 0:(i + 1) * P], op0=ALU.mult,
                                           op1=ALU.subtract).then_inc(p_split, 1)
                if s >= -T_LEAD and (not last or t < NT - T_LEAD):
                    pr, h = ((s + T_LEAD) // 2) % 2, s % 2
                    dve.wait_ge(t_hi, t + T_LEAD + 1)
                    v.scalar_tensor_tensor(out=tT[:, pr, LO, 2 * h:2 * h + 2], in0=t_ps[:, :, :], scalar=T_DOWN,
                                           in1=tT[:, pr, HI, 2 * h:2 * h + 2], op0=ALU.mult,
                                           op1=ALU.subtract).then_inc(t_split, 1)
                if norm:
                    ln_rows(k, rk, src, s + LN_LEAD >= 2)
                for m, n in terns[:1]:
                    ternary(m, n)
                if s >= 1:
                    q = (s - 1) % 2
                    v.reciprocal(rinv[:, q:q + 1], rowsum[:, q:q + 1]).then_inc(o_inv, 1)
                    dve.wait_ge(o_inv, t)
                    par = ((s - 1) // TB) % 2
                    v.tensor_scalar(osc[:, q:q + 1], rinv[:, q:q + 1], fsc[:, par:par + 1], None,
                                    ALU.mult).then_inc(o_scaled, 1)
                    dve.wait_ge(o_scaled, t)
                    dve.wait_ge(pv_mm, t)
                    dve.wait_ge(x2_stored[(s - 1) % 4], it * (BODY // 4) * 16 + ((s - 1) // 4 + 1) * 16)
                    v.scalar_tensor_tensor(out=x2_ring[:, (s - 1) % 4], in0=o_ps[:, :], scalar=osc[:, q:q + 1],
                                           in1=x_ring[:, (s - 1) % 8], op0=ALU.mult, op1=ALU.add).then_inc(o_done, 1)
                if s >= -1 and (not last or t + 1 < NT):
                    j, par = (s + 1) % TB, ((s + 1) // TB) % 2
                    dve.wait_ge(v_hi, t + 2)
                    v.scalar_tensor_tensor(out=v_s[:, par, LO, j], in0=v_ps[:, :], scalar=V_DOWN,
                                           in1=v_s[:, par, HI, j], op0=ALU.mult,
                                           op1=ALU.subtract).then_inc(v_split, 1)
                if s > 0 and (not last or t + TB < NT):
                    batch, c = it * 2 + s // TB + 1, ctx_step(s)
                    if c in (1, 2):
                        if c == 1:
                            dve.wait_ge(ctx_in, batch * 16 + 16)
                        ins = ctx_half(c - 1)
                        if c == 2:
                            ins.then_inc(ctx_max, 1)
                    if c == 4:
                        ctx_scale(batch, (s // TB + 1) % 2, batch - 1)
                    for q in CTX_SPLITS.get(c, ()):
                        ctx_lower(batch, (s // TB + 1) % 2, q)
                if last and t in TOTAL_SLOTS:
                    w = TOTAL_SLOTS[t]
                    dve.wait_ge(w_summed, (w + 1) * NW // 2)
                    v.tensor_reduce(wtot[:, w:w + 1], wsum[:, w * NW // 2:(w + 1) * NW // 2], AX.X,
                                    ALU.add).then_inc(w_total, 1)
                for m, n in terns[1:]:
                    ternary(m, n)

            def ternary(m, n):
                w = n // (NW // 2)
                th, nth = ((C_TH1, C_NTH1), (C_TH2, C_NTH2))[w]
                if n % (NW // 2) == 0:
                    dve.wait_ge(w_total_all, w + 1)
                    v.tensor_scalar(col(th), wtot[:, 2 + w:3 + w], 0.5 / (D * FC * P), 0.5e-8, ALU.mult,
                                    ALU.max).then_inc(w_thresh, 1)
                    dve.wait_ge(w_thresh, 2 * w + 1)
                    v.tensor_scalar(col(nth), col(th), -1.0, None, ALU.mult).then_inc(w_thresh, 1)
                    dve.wait_ge(w_thresh, 2 * w + 2)
                dve.wait_ge(w_loaded[m % WR], 16 * (m // WR + 1))
                if n:
                    dve.wait_ge(w_ternary, n)
                v.tensor_scalar(w_neg[:, :], w_in[:, m % WR], col(nth), None, ALU.is_lt).then_inc(w_negs, 1)
                dve.wait_ge(w_negs, n + 1)
                v.scalar_tensor_tensor(out=w_dst(n), in0=w_in[:, m % WR], scalar=col(th), in1=w_neg[:, :],
                                       op0=ALU.is_gt, op1=ALU.subtract).then_inc(w_ternary, 1)

            for s in range(FIRST_SLOT, 1):
                slot(0, s)
                if s == A_SLOT:
                    scale_wv()
                    scale_product()
                    wv_lower()
                    dve.wait_ge(ctx_in, 16)
                    ctx_half(0)
                if s == C_SLOT:
                    ctx_half(1).then_inc(ctx_max, 1)
                    scale_first_ctx()
                for q in FIRST_SPLITS.get(s, ()):
                    ctx_lower(0, 0, q)
            with dve.Fori(0, TURNS - 1) as it:
                for s in range(1, BODY + 1):
                    slot(it, s)
            for s in range(1, BODY + 1):
                slot(TURNS - 1, s, last=True)

            def hidden(F, f, bn_tile=None):
                if bn_tile is not None:
                    dve.wait_ge(bn_done, bn_tile + 1)
                dve.wait_ge(g_hi, F + 1)
                v.scalar_tensor_tensor(out=g_s[:, f % 4, LO], in0=g32[:, f % 2], scalar=col(C_SG),
                                       in1=g_s[:, f % 4, HI], op0=ALU.mult, op1=ALU.subtract).then_inc(g_split, 1)

            def group(it, gg, last=False):
                g = it * 2 + gg
                for f in range(FC):
                    F = g * FC + f
                    norm = f in LN_STEPS and (not last or F + FC < NG * FC)
                    if norm:
                        i = LN_STEPS.index(f)
                        u = ((gg + 1) % 2) * GT + i
                        k = NT + GT + g * GT + i
                        dve.wait_ge(x2_loaded[u], (it * 16 + 16) if gg == 0 else (it * 16 + 32))
                        v.bn_stats(bn6[:, i % 2], x2_in[:, u]).then_inc(bn_done, 1)
                    if not last or F + 2 < NG * FC:
                        hidden(F + 2, f + 2, k if norm else None)
                    if norm:
                        ln_variance(k, i % 2)
                        ln_rows(k, i % 2, x2_in[:, u], True)
                    if f == FC - 1:
                        for i in range(GT):
                            dve.wait_ge(y_mm, g * GT + i + 1)
                            dve.wait_ge(x2_biased, g * GT + i + 1)
                            dve.wait_ge(y_stored[i], (g + 1) * 16)
                            v.scalar_tensor_tensor(out=y_out[:, i], in0=y_ps[i], scalar=col(C_FG),
                                                   in1=x2_in[:, gg * GT + i], op0=ALU.mult,
                                                   op1=ALU.add).then_inc(y_done, 1)

            hidden(0, 0)
            hidden(1, 1)
            with dve.Fori(0, NG // 2 - 1) as it:
                group(it, 0)
                group(it, 1)
            group(NG // 2 - 1, 0, last=True)
            group(NG // 2 - 1, 1, last=True)

        @block.tensor
        def _(pe):
            mm = nc.tensor.matmul

            def product(c):
                pe.wait_ge(w_qk_in[c], 32)
                for m in range(DC):
                    last_mm = mm(a_ps[m], wqk_in[:, 0, c, m * P:(m + 1) * P], wqk_in[:, 1, c, :],
                                 start=(c == 0), stop=(c == DC - 1))
                    if c == DC - 1 and m % 2:
                        last_mm.then_inc(a_mm, 1)

            def transposes(k, r):
                pe.wait_ge(xn_lo, k + 1)
                if not isinstance(k, int) or k > 0:
                    pe.wait_ge(xT_ready, k)
                for a in (HI, LO):
                    for c in range(DC):
                        tr = nc.tensor.transpose(xT_ps[:, a, c], xn_s[:, r, a, c * P:(c + 1) * P], ident[:, :])
                tr.then_inc(x_tr, 1)

            def hidden(F, f, g):
                if f % FC == 0:
                    pe.wait_ge(xT_ready, NT + (g + 1) * GT)
                if f >= 2:
                    pe.wait_ge(g_act, F - 1)
                for a in (HI, LO):
                    for c in range(DC):
                        last_mm = mm(h_ps[f % 2], w1_s[:, c, (f % FC) * P:(f % FC + 1) * P],
                                     yT[:, (f // FC) % 2, a, c, :], start=(a == HI and c == 0),
                                     stop=(a == LO and c == DC - 1))
                last_mm.then_inc(h_mm, 1)

            def slot(it, s, last=False):
                t = it * BODY + s
                i = s % TB
                if s >= 1:
                    pe.wait_ge(p_split, t)
                    for a in (HI, LO):
                        for j in range((s - 1) % TB + 1):
                            tr = nc.tensor.transpose(pT_ps[:, a, j * P:(j + 1) * P], p_s[:, a, j * P:(j + 1) * P],
                                                     ident[:, :])
                    tr.then_inc(p_tr, 1)
                if s >= 0 and (not last or t < NT):
                    par, pr, q = (s // TB) % 2, (s // 2) % 2, s % 2
                    pe.wait_ge(t_split, t - q + 2)
                    pe.wait_ge(ctx_split, it * 8 + s // TB * 4 + i // 2 + 1)
                    if s >= 1:
                        pe.wait_ge(p_exp, t)
                    w = (i + 1) * P
                    for lo in range(0, w, 512):
                        hi = min(w, lo + 512)
                        for n, (ta, ca) in enumerate(PASSES):
                            for c in range(DC):
                                last_mm = mm(s_ps[:, lo:hi], tT[:, pr, ta, c, q * P:(q + 1) * P],
                                             ctx_s[:, par, ca, c, lo:hi], start=(n == 0 and c == 0),
                                             stop=(n == 2 and c == DC - 1))
                    last_mm.then_inc(s_mm, 1)
                if s >= -T_LEAD and (not last or t < NT - T_LEAD):
                    pr, h = ((s + T_LEAD) // 2) % 2, s % 2
                    pe.wait_ge(xT_ready, t + T_LEAD - h + 2)
                    if s == -T_LEAD:
                        pe.wait_ge(a_hi, DC)
                    else:
                        pe.wait_ge(t_split, t + T_LEAD)
                    for dd in range(2):
                        d = 2 * h + dd
                        for n, (xa, aa) in enumerate(PASSES):
                            if s == -T_LEAD and dd == 0 and aa == LO:
                                pe.wait_ge(a_split, DC)
                            for c in range(DC):
                                last_mm = mm(t_ps[:, dd], a_s[:, aa, c, d * P:(d + 1) * P], xnT[:, pr, xa, c, :],
                                             start=(n == 0 and c == 0), stop=(n == 2 and c == DC - 1))
                    last_mm.then_inc(t_mm, 1)
                if last and t == NT:
                    pe.wait_ge(w_ternary, NW)
                    hidden(0, 0, 0)
                    hidden(1, 1, 0)
                if s >= 1:
                    pe.wait_ge(pT_ready, t)
                    pe.wait_ge(v_split, t + 1 if not last or t < NT else NT)
                    if last and t == NT:
                        pe.wait_ge(o_done, NT - 1)
                    jn, par = (s - 1) % TB, ((s - 1) // TB) % 2
                    for n, (pa, va) in enumerate(PASSES):
                        for j in range(jn + 1):
                            last_mm = mm(o_ps[:, :], pT[:, pa, j * P:(j + 1) * P], v_s[:, par, va, j],
                                         start=(n == 0 and j == 0), stop=(n == 2 and j == jn))
                    last_mm.then_inc(pv_mm, 1)
                if s >= -1 and (not last or t + 1 < NT):
                    j, par = (s + 1) % TB, ((s + 1) // TB) % 2
                    pe.wait_ge(ctx_split, it * 8 + (s + 1) // TB * 4 + j // 2 + 1)
                    if s >= 0:
                        pe.wait_ge(v_split, t + 1)
                    else:
                        pe.wait_ge(wv_split, 1)
                    for n, (ca, va) in enumerate(PASSES):
                        for c in range(DC):
                            last_mm = mm(v_ps[:, :], ctx_s[:, par, ca, c, j * P:(j + 1) * P], wv_s[:, va, c, :],
                                         start=(n == 0 and c == 0), stop=(n == 2 and c == DC - 1))
                    last_mm.then_inc(v_mm, 1)
                if s >= -XT_LEAD and (not last or t + XT_LEAD < NT + GT):
                    transposes(t + XT_LEAD, (s + XT_LEAD) % 2)

            for s in range(FIRST_SLOT, 1):
                slot(0, s)
                for c in PRODUCTS.get(s, ()):
                    product(c)
                if s == FIRST_SLOT:
                    pe.wait_ge(consts, 5)
            with pe.Fori(0, TURNS - 1) as it:
                for s in range(1, BODY + 1):
                    slot(it, s)
            for s in range(1, BODY + 1):
                slot(TURNS - 1, s, last=True)

            def group(it, gg, last=False):
                g = it * 2 + gg
                for f in range(FC):
                    F = g * FC + f
                    if not last or F + 2 < NG * FC:
                        hidden(F + 2, gg * FC + f + 2, g + (f + 2) // FC)
                    pe.wait_ge(g_split, F + 1)
                    for i in range(GT):
                        if f == 0:
                            pe.wait_ge(y_done, g * GT + i + 1)
                        for a in (HI, LO):
                            last_mm = mm(y_ps[i], g_s[:, f % 4, a, i * P:(i + 1) * P], w2_s[:, f, :],
                                         start=(f == 0 and a == HI), stop=(f == FC - 1 and a == LO))
                        if f == FC - 1:
                            last_mm.then_inc(y_mm, 1)
                    if f in XT_STEPS and (not last or F + FC < NG * FC):
                        i = XT_STEPS.index(f)
                        transposes(NT + GT + g * GT + i, i % 2)

            with pe.Fori(0, NG // 2 - 1) as it:
                group(it, 0)
                group(it, 1)
            group(NG // 2 - 1, 0, last=True)
            group(NG // 2 - 1, 1, last=True)


def kernel(x, ctx_1024, g_xattn, g_ffn, L0_xattn_w_q, L0_xattn_w_k, L0_xattn_w_v, L0_ffn_W1, L0_ffn_b1,
           L0_ffn_W2, L0_ffn_b2):
    import numpy as np
    import concourse.bacc as bacc
    from concourse.bass_utils import run_bass_kernel_spmd

    B, S, D = x.shape
    C = D // P

    def chunks(a):
        return np.ascontiguousarray(a.reshape(a.shape[0] // P, P, -1).transpose(1, 0, 2))

    arrays = {
        "x": np.ascontiguousarray(np.asarray(x).reshape(B * S, D)),
        "ctxT": np.ascontiguousarray(np.asarray(ctx_1024).transpose(0, 2, 1).reshape(B, C, P, S).transpose(0, 2, 1, 3)),
        "g_xattn": np.asarray(g_xattn),
        "g_ffn": np.asarray(g_ffn),
        "wqT": chunks(np.asarray(L0_xattn_w_q).T),
        "wkT": chunks(np.asarray(L0_xattn_w_k).T),
        "wv": chunks(np.asarray(L0_xattn_w_v)),
        "w1T": chunks(np.asarray(L0_ffn_W1).T).reshape(P, -1),
        "b1c": np.ascontiguousarray(np.asarray(L0_ffn_b1).reshape(-1, P).T),
        "w2T": chunks(np.asarray(L0_ffn_W2).T).reshape(P, -1),
        "b2": np.asarray(L0_ffn_b2),
    }
    nc = bacc.Bacc("TRN2", target_bir_lowering=False, num_devices=1)
    args = {n: nc.dram_tensor(f"in_{n}", a.shape, mybir.dt.from_np(a.dtype), kind="ExternalInput").ap()
            for n, a in arrays.items()}
    out = nc.dram_tensor("out_y", (B * S, D), F32, kind="ExternalOutput").ap()
    gated_block(nc, *args.values(), out)
    r = run_bass_kernel_spmd(nc, [{f"in_{n}": a for n, a in arrays.items()}], core_ids=[0])
    return r.results[0]["out_y"].reshape(B, S, D)
```
